# Optimizing a Trainium2 kernel written in Bass

```python
import numpy as np
import jax
import jax.numpy as jnp

def _softmax(x, axis=-1):
    return jax.nn.softmax(x, axis=axis)

def _gelu(x):
    return jax.nn.gelu(x, approximate=True)

def _silu(x):
    return jax.nn.silu(x)

def _sigmoid(x):
    return jax.nn.sigmoid(x)

def _layernorm(x, axis=-1, eps=1e-05):
    m = jnp.mean(x, axis=axis, keepdims=True)
    v = jnp.var(x, axis=axis, keepdims=True)
    return (x - m) / jnp.sqrt(v + eps)

def _scatter_add(tgt, idx, src, axis=0):
    return tgt.at[idx].add(src)

def _segment_sum(src, seg, n):
    return jax.ops.segment_sum(src, seg, n)
kernel_name = 'mk_flamingo_gated_d1_seqx_r4_29f8eb'

def setup_inputs(seed: int=0):
    np.random.seed(seed)
    _w = jnp.asarray

    def _rec_inputs():
        import jax
        import jax.numpy as jnp
        _rk = jax.random.key(seed)
        x = -0.0003929 + 0.9999 * jax.random.normal(jax.random.fold_in(_rk, 1), (4, 512, 256), jnp.float32)
        _lenS = 512 - jax.random.randint(jax.random.fold_in(_rk, 7), (4,), 0, max(1, 512 // 4) + 1, jnp.int32)
        _lenS2 = 512 - jax.random.randint(jax.random.fold_in(_rk, 8), (4,), 0, max(1, 512 // 4) + 1, jnp.int32)
        _ctx_1024P = jax.random.normal(jax.random.fold_in(_rk, 11), (4, 16, 256), jnp.float32)
        _ctx_1024c = jax.random.dirichlet(jax.random.fold_in(_rk, 511), 0.3 * jnp.ones((16,), jnp.float32), (4, 512))
        _ctx_1024t = jnp.einsum('bsk,bkd->bsd', _ctx_1024c, _ctx_1024P)
        _ctx_1024t = _ctx_1024t * jax.lax.rsqrt(jnp.mean(jnp.square(_ctx_1024t)) + 1e-12) * 0.953939
        ctx_1024 = 2.81802e-05 + 1.00001 * (_ctx_1024t + 0.3 * jax.random.normal(jax.random.fold_in(_rk, 611), (4, 512, 256), jnp.float32))
        _g = jax.random.normal(jax.random.fold_in(_rk, 9001), (2, 1), jnp.float32)
        _g = jnp.sign(_g) * jnp.maximum(jnp.abs(_g), 1.0) + (_g == 0) * 1.0
        g_xattn = _g[0]
        g_ffn = _g[1]
        return (x, ctx_1024, g_xattn, g_ffn)
    x, ctx_1024, g_xattn, g_ffn = _rec_inputs()

    def _L0_xattn_setup():
        import math
        import jax, jax.numpy as jnp
        import numpy as np
        D_MODEL = 256
        N_HEADS = 16
        D_K = D_MODEL // N_HEADS

        def _autocorr_forward(queries, keys, values, Wq, bq, Wk, bk, Wv, bv, Wo, bo):
            B, L, D = queries.shape
            H, dk = (N_HEADS, D_K)
            q = (queries @ Wq.T + bq).reshape(B, L, H, dk)
            k = (keys @ Wk.T + bk).reshape(B, L, H, dk)
            v = (values @ Wv.T + bv).reshape(B, L, H, dk)
            qf = jnp.fft.rfft(q, axis=1)
            kf = jnp.fft.rfft(k, axis=1)
            corr = jnp.fft.irfft(qf * jnp.conj(kf), n=L, axis=1).mean(axis=-1)
            corr = corr.transpose(0, 2, 1)
            topk = min(max(1, int(math.log(L))), L)
            weights, delays = jax.lax.top_k(corr, topk)
            w = jax.nn.softmax(weights, axis=-1)
            idx = (jnp.arange(L)[None, None, None, :] - delays[..., None]) % L
            v_h = v.transpose(0, 2, 1, 3)
            gathered = jnp.take_along_axis(v_h[:, :, None], idx[..., None], axis=3)
            out = (w[..., None, None] * gathered).sum(axis=2)
            out = out.transpose(0, 2, 1, 3).reshape(B, L, D)
            return out @ Wo.T + bo
        key = jax.random.key(seed)
        ks = jax.random.split(key, 12)
        B, L, D = (8, 512, D_MODEL)
        scale = 1.0 / math.sqrt(D)
        inp = {'queries': jax.random.normal(ks[0], (B, L, D), jnp.float32), 'keys': jax.random.normal(ks[1], (B, L, D), jnp.float32), 'values': jax.random.normal(ks[2], (B, L, D), jnp.float32), 'Wq': jax.random.normal(ks[3], (D, D), jnp.float32) * scale, 'bq': jnp.zeros((D,), jnp.float32), 'Wk': jax.random.normal(ks[4], (D, D), jnp.float32) * scale, 'bk': jnp.zeros((D,), jnp.float32), 'Wv': jax.random.normal(ks[5], (D, D), jnp.float32) * scale, 'bv': jnp.zeros((D,), jnp.float32), 'Wo': jax.random.normal(ks[6], (D, D), jnp.float32) * scale, 'bo': jnp.zeros((D,), jnp.float32)}
        return inp
    _L0_xattn_all = _L0_xattn_setup()
    _L0_xattn_in = {k: v for k, v in _L0_xattn_all.items() if k in ('Wq', 'bq', 'Wk', 'bk', 'Wv', 'bv', 'Wo', 'bo')}
    del _L0_xattn_all

    def _L0_ffn_setup():
        import jax, jax.numpy as jnp
        import numpy as np
        B, S, D, E = (2, 512, 256, 8)
        key = jax.random.key(seed)
        ks = jax.random.split(key, 5)
        x = jax.random.normal(ks[0], (B, S, D), dtype=jnp.float32)
        router_w = jax.random.normal(ks[1], (E, D), dtype=jnp.float32) * 0.02
        router_b = jnp.zeros((E,), dtype=jnp.float32)
        expert_w = jax.random.normal(ks[2], (E, D, D), dtype=jnp.float32) * 0.02
        expert_b = jnp.zeros((E, D), dtype=jnp.float32)
        return {'x': x, 'router_w': router_w, 'router_b': router_b, 'expert_w': expert_w, 'expert_b': expert_b}
    _L0_ffn_all = _L0_ffn_setup()
    _L0_ffn_in = {k: v for k, v in _L0_ffn_all.items() if k in ('router_w', 'router_b', 'expert_w', 'expert_b')}
    del _L0_ffn_all
    return {'x': x, 'ctx_1024': ctx_1024, 'g_xattn': g_xattn, 'g_ffn': g_ffn, 'L0_xattn_Wq': _L0_xattn_in['Wq'], 'L0_xattn_bq': _L0_xattn_in['bq'], 'L0_xattn_Wk': _L0_xattn_in['Wk'], 'L0_xattn_bk': _L0_xattn_in['bk'], 'L0_xattn_Wv': _L0_xattn_in['Wv'], 'L0_xattn_bv': _L0_xattn_in['bv'], 'L0_xattn_Wo': _L0_xattn_in['Wo'], 'L0_xattn_bo': _L0_xattn_in['bo'], 'L0_ffn_router_w': _L0_ffn_in['router_w'], 'L0_ffn_router_b': _L0_ffn_in['router_b'], 'L0_ffn_expert_w': _L0_ffn_in['expert_w'], 'L0_ffn_expert_b': _L0_ffn_in['expert_b']}

def reference(x, ctx_1024, g_xattn, g_ffn, L0_xattn_Wq, L0_xattn_bq, L0_xattn_Wk, L0_xattn_bk, L0_xattn_Wv, L0_xattn_bv, L0_xattn_Wo, L0_xattn_bo, L0_ffn_router_w, L0_ffn_router_b, L0_ffn_expert_w, L0_ffn_expert_b):
    import jax
    import jax.numpy as jnp

    def _L0_xattn_ref(queries, keys, values, Wq, bq, Wk, bk, Wv, bv, Wo, bo):
        import math
        import jax, jax.numpy as jnp
        import numpy as np
        D_MODEL = 256
        N_HEADS = 16
        D_K = D_MODEL // N_HEADS

        def _autocorr_forward(queries, keys, values, Wq, bq, Wk, bk, Wv, bv, Wo, bo):
            B, L, D = queries.shape
            H, dk = (N_HEADS, D_K)
            q = (queries @ Wq.T + bq).reshape(B, L, H, dk)
            k = (keys @ Wk.T + bk).reshape(B, L, H, dk)
            v = (values @ Wv.T + bv).reshape(B, L, H, dk)
            qf = jnp.fft.rfft(q, axis=1)
            kf = jnp.fft.rfft(k, axis=1)
            corr = jnp.fft.irfft(qf * jnp.conj(kf), n=L, axis=1).mean(axis=-1)
            corr = corr.transpose(0, 2, 1)
            topk = min(max(1, int(math.log(L))), L)
            weights, delays = jax.lax.top_k(corr, topk)
            w = jax.nn.softmax(weights, axis=-1)
            idx = (jnp.arange(L)[None, None, None, :] - delays[..., None]) % L
            v_h = v.transpose(0, 2, 1, 3)
            gathered = jnp.take_along_axis(v_h[:, :, None], idx[..., None], axis=3)
            out = (w[..., None, None] * gathered).sum(axis=2)
            out = out.transpose(0, 2, 1, 3).reshape(B, L, D)
            return out @ Wo.T + bo
        return _autocorr_forward(queries, keys, values, Wq, bq, Wk, bk, Wv, bv, Wo, bo)

    def _L0_ffn_ref(x, router_w, router_b, expert_w, expert_b):
        import jax, jax.numpy as jnp
        import numpy as np
        B, S, D, E = (2, 512, 256, 8)
        logits = jnp.einsum('bsd,ed->bse', x, router_w) + router_b
        probs = jax.nn.softmax(logits, axis=-1)
        weights = jnp.max(probs, axis=-1)
        top1 = jnp.argmax(probs, axis=-1)
        y_all = jnp.einsum('bsd,eod->bseo', x, expert_w) + expert_b
        y = jnp.take_along_axis(y_all, top1[:, :, None, None], axis=2)[:, :, 0, :]
        out = y * weights[:, :, None]
        return out
    x = x + jnp.tanh(g_xattn[0]) * _L0_xattn_ref(_layernorm(x, axis=-1), ctx_1024, ctx_1024, L0_xattn_Wq, L0_xattn_bq, L0_xattn_Wk, L0_xattn_bk, L0_xattn_Wv, L0_xattn_bv, L0_xattn_Wo, L0_xattn_bo)
    x = x + jnp.tanh(g_ffn[0]) * _L0_ffn_ref(_layernorm(x, axis=-1), L0_ffn_router_w, L0_ffn_router_b, L0_ffn_expert_w, L0_ffn_expert_b)
    return x

_drawn_inputs = setup_inputs


def setup_inputs(seed=0):
    import zlib

    import numpy as np

    out = dict(_drawn_inputs(seed))
    spreads = {'L0_xattn_bq': (0.0, 0.8),
     'L0_xattn_bk': (0.0, 0.8),
     'L0_xattn_bv': (0.0, 0.1),
     'L0_xattn_bo': (0.0, 0.1),
     'L0_ffn_router_b': (0.0, 0.318),
     'L0_ffn_expert_b': (0.0, 0.487)}
    factors = {}
    for name, (base, spread) in spreads.items():
        noise = np.random.default_rng([zlib.crc32(name.encode()), seed]).standard_normal(out[name].shape)
        drawn = base * np.exp(spread * noise) if base else spread * noise
        out[name] = jnp.asarray(drawn.astype(out[name].dtype))
    for name, factor in factors.items():
        out[name] = (out[name] * factor).astype(out[name].dtype)
    return out
```

```python
from contextlib import ExitStack

import numpy as np

import concourse.bass as bass
from concourse import mybir

P = 128
B, L, D = 4, 512, 256
H, DK = 16, 16
E = 8
S = L // P
C = D // P
G = 4
J = 64
HC = P // DK
ROWS = B * H
TOPK = 6
EPS = 1e-5
LEAD = 2

PER_BATCH = dict(
    stats_ok=S, aggr_ok=S, var_ok=1, ln_ok=1, rs_ok=1, newton_ok=3, xn_ok=S, half_ok=1, xc_ok=3,
    chalf_ok=1, cc_ok=3, xspec_done=C, cspec_done=C, xf_ok=C, cf_ok=C, q_done=C, k_done=C, k_ok=C,
    m_ok=3 * C, prod0_ok=2, prod_ok=1, sum_done=1, v_done=C, v_ok=C, wstage_ok=1, wspec_done=C,
    n_ok=3 * C, vp0_ok=2, vp_ok=1, y_done=2, y_ok=2, even_done=1, odd_done=1, res1_ok=2, res2_ok=2,
    stats2_ok=S, aggr2_ok=S, var2_ok=1, ln2_ok=1, rs2_ok=1, newton2_ok=3, xn2_ok=S)
PER_TILE = dict(
    turned_done=1, xt_ok=1, logit_done=1, lg_ok=1, nmax_ok=1, prob_ok=1, rden_ok=1, cw_ok=1,
    first_ok=1, pick_ok=1, big_ok=1, c_ok=1, ct_done=1, ct_ok=1, ebias_done=1, acc_ok=1,
    expert_done=E // 2, sel_ok=E)
PER_LOAD = dict(x_in0=16, x_in1=16, c_in0=16, c_in1=16, out_done0=16, out_done1=16)
PER_ROUND = {**PER_BATCH, **PER_TILE, **PER_LOAD}
ONCE = """passed table_in w_in row_in consts_in gates_in late_in gate_ok cspec_ok corr_done corr_ok top_ok
    topi_ok lasti_ok wmax_ok exp_ok keep1_ok keep2_ok keep3_ok wsum_ok wr_ok w_ok wt_done wt_ok
    whalf_ok wc_ok""".split()
WITH_LEAD = dict(
    tensor=("xspec_done", "cspec_done", "q_done", "sum_done", "wspec_done", "y_done", "odd_done",
            "turned_done", "ct_done", "ebias_done", "expert_done"),
    scalar=("cf_ok", "k_ok", "v_ok", "y_ok", "xt_ok"),
    vector=("m_ok", "n_ok", "res1_ok", "res2_ok", "xn2_ok", "acc_ok", "sel_ok"),
    gpsimd=("prod_ok", "vp_ok"),
    sync=("out_done0", "out_done1"))
LED = {n for names in WITH_LEAD.values() for n in names}


def after(name, r, k=None):
    n = PER_ROUND[name]
    return r * n + ((LEAD * n if name in LED else 0) + (n if k is None else k))

F32 = mybir.dt.float32
U32 = mybir.dt.uint32
ALU = mybir.AluOpType
ACT = mybir.ActivationFunctionType
AX_X = mybir.AxisListType.X


def dft_tables():
    t = np.arange(L)
    j = np.arange(J)
    f = [4 * j, 4 * j + 2, 4 * j + 1, 4 * j + 3]

    def angle(times, freqs):
        return 2 * np.pi * ((times[:, None] * freqs[None, :]) % L) / L

    q = t[:P]
    forward = []
    for g in (0, 1):
        a = angle(q, f[g])
        re, im = np.cos(a), -np.sin(a)
        if g == 0:
            im[:, 0] = np.where(q % 2 == 0, 1.0, -1.0)
        forward += [re, im]
    for g in (2, 3):
        a = angle(q, f[g])
        forward += [np.cos(a), -np.sin(a)]
    for g, sign in ((2, -1.0), (3, 1.0)):
        a = angle(q, f[g])
        forward += [sign * np.sin(a), sign * np.cos(a)]
    inverse = np.zeros((2, J, G, L))
    for g in range(G):
        a = angle(t, f[g]).T
        inverse[0, :, g] = 2.0 * np.cos(a) / L
        inverse[1, :, g] = -2.0 * np.sin(a) / L
    inverse[0, 0, 0] = 1.0 / L
    inverse[1, 0, 0] = np.where(t % 2 == 0, 1.0, -1.0) / L
    return (np.concatenate(forward, 1).astype(np.float32),
            inverse.reshape(P, G * L).astype(np.float32))


def build(nc, x, ctx, g_xattn, g_ffn, wq, wk, wv, wo, bq, bk, bv, bo, rw, rb, ew, eb,
          fwd_table, inv_table, head_ones, ident, const_row, counts, out):
    es = ExitStack()
    with es:
        def sb(name, shape, dt=F32):
            return es.enter_context(nc.sbuf_tensor(name, shape, dt))

        def sem(name):
            return es.enter_context(nc.semaphore(name))

        bank = [es.enter_context(nc.psum_tensor(f"bank{n}", [P, 512], F32)) for n in range(8)]
        spectrum_ps = bank[0:2]
        q_ps = bank[2:4]
        k_ps = bank[4:6]
        corr_spec_ps = bank[6]
        corr_ps = bank[7]
        v_ps = bank[2:4]
        wt_ps = bank[0]
        wspec_ps = bank[0:2]
        y_ps = bank[2:4]
        even_ps = bank[0]
        odd_ps = bank[1]
        expert_ps = bank[2:6]
        turned_ps = bank[6]
        logit_ps = bank[7][:, 0:E]
        ct_ps = bank[7][0:E, 16:16 + P]
        ebias_ps = bank[7][:, 256:256 + D]

        fwd = sb("fwd", [P, 6 * P])
        inv = sb("inv", [P, G, L])
        hones = sb("hones", [P, HC])
        idn = sb("idn", [P, P])
        crow = sb("crow", [1, P + P])
        cnt = sb("cnt", [P, L + E])
        wq_sb, wk_sb, wv_sb, wo_sb = (sb(n, [P, C, D]) for n in ("wq_sb", "wk_sb", "wv_sb", "wo_sb"))
        bias_sb = sb("bias_sb", [1, 4, D])
        rw_sb = sb("rw_sb", [P, C, E])
        rb_sb = sb("rb_sb", [1, E])
        ew_sb = sb("ew_sb", [P, C, E, D])
        eb_sb = sb("eb_sb", [E, D])
        gates = sb("gates", [P, 2])
        tg = sb("tg", [P, 3])

        x_sb = sb("x_sb", [P, B, S, D])
        ctx_sb = sb("ctx_sb", [P, B, S, D])
        x2_sb = sb("x2_sb", [P, 2, S, D])
        stats = sb("stats", [P, S, 6])
        mv = sb("mv", [P, S, 2])
        root = sb("root", [P, 4, S])
        xn = sb("xn", [P, S, D])
        half = sb("half", [P, 2, D])
        chalf = sb("chalf", [P, 2, D])
        xc = sb("xc", [P, 2, 4, D])
        cc = sb("cc", [P, 2, 4, D])
        xf = sb("xf", [P, 2, C, L])
        cf = sb("cf", [P, B, C, L])
        k_sb = sb("k_sb", [P, 2, C, L])
        m1 = sb("m1", [P, 2, C, G, 2, J])
        m2 = sb("m2", [P, 2, C, G, 2, J])
        prod = sb("prod", [P, 2, C, G, 2, J])
        v_sb = sb("v_sb", [P, B, C, L])
        corr_spec = sb("corr_spec", [P, G, ROWS])
        corr = sb("corr", [ROWS, L])
        top = sb("top", [ROWS, 8])
        topi = sb("topi", [ROWS, 8], U32)
        last = sb("last", [ROWS, 4])
        ex = sb("ex", [ROWS, L])
        keep = sb("keep", [ROWS, L])
        w_sb = sb("w_sb", [ROWS, L])
        wt = sb("wt", [P, S, ROWS])
        whalf = sb("whalf", [P, 2, ROWS])
        wc = sb("wc", [P, 4, ROWS])
        wstage = k_sb[:, :, :, :].rearrange("p b c l -> p b (c l)").rearrange("p b (k d) -> p b k d", k=4)
        y_sb = cc
        xn2 = xc
        xt = sb("xt", [P, 2, C, P])
        lg = sb("lg", [P, 2, 5, E])
        col = sb("col", [P, 2, 8])
        c_sb = sb("c_sb", [P, 2, E])
        ct = sb("ct", [E, 2, P])
        acc = sb("acc", [P, 2, D])

        s = {n: sem(n) for n in (*PER_ROUND, *ONCE)}
        block = es.enter_context(nc.Block())

        def wait(eng, name, r, k=None):
            eng.wait_ge(s[name], after(name, r, k))

        def wait_alone(eng, name, r):
            wait(eng, name, r)
            eng.sem_inc(s["passed"], 1)

        def give_lead(eng, kind):
            for n in WITH_LEAD[kind]:
                eng.sem_inc(s[n], LEAD * PER_ROUND[n])

        @block.sync
        def _(sp):
            give_lead(sp, "sync")
            with nc.sync.Fori(0, B // 2) as i:
                for p in range(2):
                    b = i * 2 + p
                    sp.dma_start(x_sb[:, b], x[b].rearrange("(s p) d -> p s d", p=P)).then_inc(s[f"x_in{p}"], 16)
                    sp.dma_start(ctx_sb[:, b], ctx[b].rearrange("(s p) d -> p s d", p=P)).then_inc(s[f"c_in{p}"], 16)
                for p in range(2):
                    wait(sp, f"x_in{p}", i)
                    wait_alone(sp, f"c_in{p}", i)
            sp.dma_start(ew_sb[:, :, :, :], ew).then_inc(s["late_in"], 16)
            sp.dma_start(rw_sb[:, :, :], rw).then_inc(s["late_in"], 16)
            sp.dma_start(rb_sb[:, :], rb).then_inc(s["late_in"], 16)
            sp.dma_start(eb_sb[:, :], eb).then_inc(s["late_in"], 16)
            with nc.sync.Fori(0, B // 2) as i:
                for p in range(2):
                    for t in range(S):
                        n = i * 2 * S + (p * S + t)
                        wait(sp, "sel_ok", n)
                        sp.dma_start(out[i * 2 + p, t * P:(t + 1) * P, :], acc[:, t % 2]).then_inc(s[f"out_done{t % 2}"], 16)
            for q in range(2):
                wait(sp, f"out_done{q}", B * S // 2 - 1)

        def combine(pool, b, p, made, mid, done, op_re, op_im):
            wait(pool, made, b)
            a = m1[:, p].rearrange("p c g r j -> p (c g) r j")
            m = m2[:, p].rearrange("p c g r j -> p (c g) r j")
            o = prod[:, p].rearrange("p c g r j -> p (c g) r j")
            pool.tensor_tensor(o[:, :, 0], a[:, :, 0], a[:, :, 1], op_re).then_inc(s[mid], 1)
            pool.tensor_tensor(o[:, :, 1], m[:, :, 1], m[:, :, 0], op_im).then_inc(s[mid], 1)
            wait_alone(pool, mid, b)
            pool.tensor_copy(prod[:, p, :, 0, :, 0], m1[:, p, :, 0, :, 0]).then_inc(s[done], 1)

        @block.gpsimd
        def _(pool):
            give_lead(pool, "gpsimd")
            with nc.gpsimd.Fori(0, B // 2) as i:
                for p in range(2):
                    b = i * 2 + p
                    wait(pool, f"c_in{p}", i)
                    wait(pool, "cspec_done", b - 2)
                    pool.tensor_tensor(chalf[:, :, :], ctx_sb[:, b, 0:2], ctx_sb[:, b, 2:4], ALU.add).then_inc(s["chalf_ok"], 1)
                    pool.tensor_tensor(cc[:, p, 2:4], ctx_sb[:, b, 0:2], ctx_sb[:, b, 2:4], ALU.subtract).then_inc(s["cc_ok"], 1)
                    wait(pool, "chalf_ok", b)
                    pool.tensor_tensor(cc[:, p, 0], chalf[:, 0], chalf[:, 1], ALU.add).then_inc(s["cc_ok"], 1)
                    pool.tensor_tensor(cc[:, p, 1], chalf[:, 0], chalf[:, 1], ALU.subtract).then_inc(s["cc_ok"], 1)
                    wait(pool, "sum_done", b - 2)
                    combine(pool, b, p, "m_ok", "prod0_ok", "prod_ok", ALU.add, ALU.subtract)
                    wait(pool, "cc_ok", b)
            pool.wait_ge(s["wc_ok"], 3)
            with nc.gpsimd.Fori(0, B // 2) as i:
                for p in range(2):
                    b = i * 2 + p
                    wait_alone(pool, "wspec_done", b - 2)
                    pool.tensor_copy(wstage[:, p].rearrange("p k (h r) -> p k h r", r=DK),
                                     wc[:, :, bass.ds(b * H, H)].unsqueeze(3).to_broadcast([P, 4, H, DK])
                                     ).then_inc(s["wstage_ok"], 1)
                    wait(pool, "y_done", b - 2)
                    combine(pool, b, p, "n_ok", "vp0_ok", "vp_ok", ALU.subtract, ALU.add)

        @block.scalar
        def _(act):
            give_lead(act, "scalar")
            act.dma_start(fwd[:, :], fwd_table).then_inc(s["table_in"], 16)
            act.dma_start(gates[:, 0:1], g_xattn.partition_broadcast(P)).then_inc(s["gates_in"], 16)
            act.dma_start(gates[:, 1:2], g_ffn.partition_broadcast(P)).then_inc(s["gates_in"], 16)
            act.dma_start(wq_sb[:, :, :], wq).then_inc(s["w_in"], 16)
            act.dma_start(wk_sb[:, :, :], wk).then_inc(s["w_in"], 16)
            for n, bias in enumerate((bq, bk, bv, bo)):
                act.dma_start(bias_sb[:, n], bias).then_inc(s["row_in"], 16)
            act.dma_start(crow[:, :], const_row).then_inc(s["row_in"], 16)
            act.dma_start(hones[:, :], head_ones).then_inc(s["consts_in"], 16)
            act.dma_start(idn[:, :], ident).then_inc(s["consts_in"], 16)
            act.dma_start(cnt[:, :], counts).then_inc(s["consts_in"], 16)
            act.dma_start(inv[:, :, :], inv_table.rearrange("p (g t) -> p g t", g=G)).then_inc(s["consts_in"], 16)
            act.dma_start(wv_sb[:, :, :], wv).then_inc(s["consts_in"], 16)
            act.dma_start(wo_sb[:, :, :], wo).then_inc(s["consts_in"], 16)
            act.wait_ge(s["gates_in"], 32)
            act.activation(tg[:, 0:2], gates[:, :], ACT.Tanh).then_inc(s["gate_ok"], 1)
            act.wait_ge(s["gate_ok"], 1)
            act.mul(tg[:, 2:3], tg[:, 0:1], -1.0).then_inc(s["gate_ok"], 1)
            act.preload_act_table_set("natural_log_exp_and_others")

            def log_root(b, var_ok, ln_ok, rs_ok):
                wait(act, var_ok, b)
                act.activation(root[:, 1], root[:, 0], ACT.Ln).then_inc(s[ln_ok], 1)
                wait(act, ln_ok, b)
                act.activation(root[:, 2], root[:, 1], ACT.Exp, scale=-0.5).then_inc(s[rs_ok], 1)

            with nc.scalar.Fori(0, B // 2) as i:
                for p in range(2):
                    b = i * 2 + p
                    log_root(b, "var_ok", "ln_ok", "rs_ok")
                    wait(act, "q_done", b - 2)
                    for c in range(C):
                        wait(act, "xspec_done", b, c + 1)
                        act.copy(xf[:, p, c], spectrum_ps[c][:, :]).then_inc(s["xf_ok"], 1)
                    for c in range(C):
                        wait(act, "cspec_done", b, c + 1)
                        act.copy(cf[:, b, c], spectrum_ps[c][:, :]).then_inc(s["cf_ok"], 1)
                    wait(act, "m_ok", b - 2)
                    for c in range(C):
                        wait(act, "k_done", b, c + 1)
                        act.copy(k_sb[:, p, c], k_ps[c][:, :]).then_inc(s["k_ok"], 1)
            act.wait_ge(s["top_ok"], 1)
            act.mul(last[:, 1:2], top[:, 0:1], -1.0 / DK).then_inc(s["wmax_ok"], 1)
            act.wait_ge(s["wmax_ok"], 1)
            act.activation(ex[:, :], corr[:, :], ACT.Exp, bias=last[:, 1:2], scale=1.0 / DK).then_inc(s["exp_ok"], 1)
            with nc.scalar.Fori(0, B) as b:
                for c in range(C):
                    wait(act, "v_done", b, c + 1)
                    act.copy(v_sb[:, b, c], v_ps[c][:, :]).then_inc(s["v_ok"], 1)
            with nc.scalar.Fori(0, B // 2) as i:
                for p in range(2):
                    b = i * 2 + p
                    wait(act, "odd_done", b - 2)
                    for h in range(2):
                        wait(act, "y_done", b, h + 1)
                        act.copy(y_sb[:, p, 2 * h:2 * h + 2], y_ps[h][:, :].rearrange("p (g d) -> p g d", g=2)).then_inc(s["y_ok"], 1)
                    log_root(b, "var2_ok", "ln2_ok", "rs2_ok")
                    for t in range(S):
                        n, q = b * S + t, t % 2
                        wait(act, "turned_done", n)
                        wait(act, "expert_done", n - 2)
                        act.copy(xt[:, q], turned_ps[:, 0:D].rearrange("p (c t) -> p c t", c=C)).then_inc(s["xt_ok"], 1)
                        wait(act, "nmax_ok", n)
                        act.activation(lg[:, q, 1], lg[:, q, 0], ACT.Exp, bias=col[:, q, 0:1], accum_out=col[:, q, 1:2]).then_inc(s["prob_ok"], 1)
                        wait(act, "ct_done", n)
                        wait(act, "ebias_done", n - 2)
                        act.copy(ct[:, q], ct_ps).then_inc(s["ct_ok"], 1)

        @block.vector
        def _(dve):
            give_lead(dve, "vector")

            def statistics(src, b, stats_ok, aggr_ok, var_ok, rs_ok, newton_ok):
                for t in range(S):
                    dve.bn_stats(stats[:, t], src(t)).then_inc(s[stats_ok], 1)
                wait_alone(dve, stats_ok, b)
                for t in range(S):
                    dve.bn_aggr(mv[:, t], stats[:, t]).then_inc(s[aggr_ok], 1)
                wait(dve, aggr_ok, b)
                dve.tensor_scalar(root[:, 0], mv[:, :, 1], EPS, None, ALU.add).then_inc(s[var_ok], 1)
                wait(dve, rs_ok, b)
                dve.scalar_tensor_tensor(root[:, 1], root[:, 2], -0.5, root[:, 2], ALU.mult, ALU.mult).then_inc(s[newton_ok], 1)
                wait(dve, newton_ok, b, 1)
                dve.tensor_tensor(root[:, 1], root[:, 1], root[:, 0], ALU.mult).then_inc(s[newton_ok], 1)
                wait(dve, newton_ok, b, 2)
                dve.scalar_tensor_tensor(root[:, 3], root[:, 1], 1.5, root[:, 2], ALU.add, ALU.mult).then_inc(s[newton_ok], 1)
                wait(dve, newton_ok, b, 3)

            def products(p, c, a_ps, k, done):
                a = a_ps[:, :].rearrange("p (g r j) -> p g r j", g=G, r=2)
                k = k.rearrange("p (g r j) -> p g r j", g=G, r=2)
                dve.tensor_tensor(m1[:, p, c], a, k, ALU.mult).then_inc(s[done], 1)
                dve.tensor_tensor(m2[:, p, c, :, 0], a[:, :, 0], k[:, :, 1], ALU.mult).then_inc(s[done], 1)
                dve.tensor_tensor(m2[:, p, c, :, 1], a[:, :, 1], k[:, :, 0], ALU.mult).then_inc(s[done], 1)

            with nc.vector.Fori(0, B // 2) as i:
                for p in range(2):
                    b = i * 2 + p
                    wait(dve, f"x_in{p}", i)
                    statistics(lambda t: x_sb[:, b, t], b, "stats_ok", "aggr_ok", "var_ok", "rs_ok", "newton_ok")
                    for t in range(S):
                        dve.tensor_scalar(xn[:, t], x_sb[:, b, t], mv[:, t, 0:1], root[:, 3, t:t + 1],
                                          ALU.subtract, ALU.mult).then_inc(s["xn_ok"], 1)
                    wait(dve, "xn_ok", b)
                    wait(dve, "xspec_done", b - 2)
                    dve.tensor_tensor(half[:, :, :], xn[:, 0:2], xn[:, 2:4], ALU.add).then_inc(s["half_ok"], 1)
                    dve.tensor_tensor(xc[:, p, 2:4], xn[:, 0:2], xn[:, 2:4], ALU.subtract).then_inc(s["xc_ok"], 1)
                    wait(dve, "half_ok", b)
                    dve.tensor_tensor(xc[:, p, 0], half[:, 0], half[:, 1], ALU.add).then_inc(s["xc_ok"], 1)
                    dve.tensor_tensor(xc[:, p, 1], half[:, 0], half[:, 1], ALU.subtract).then_inc(s["xc_ok"], 1)
                    wait(dve, "xc_ok", b)
                    wait(dve, "prod_ok", b - 2)
                    for c in range(C):
                        wait(dve, "q_done", b, c + 1)
                        wait(dve, "k_ok", b, c + 1)
                        products(p, c, q_ps[c], k_sb[:, p, c], "m_ok")
            wait(dve, "sum_done", B - 1)
            dve.tensor_copy(corr_spec[:, :, :], corr_spec_ps[:, 0:G * ROWS].rearrange("p (g r) -> p g r", g=G)).then_inc(s["cspec_ok"], 1)
            dve.wait_ge(s["corr_done"], 1)
            dve.tensor_copy(corr[:, :], corr_ps[0:ROWS, :]).then_inc(s["corr_ok"], 1)
            dve.wait_ge(s["corr_ok"], 1)
            dve.max(top[:, :], corr[:, :]).then_inc(s["top_ok"], 1)
            dve.wait_ge(s["top_ok"], 1)
            dve.max_index(topi[:, :], top[:, :], corr[:, :]).then_inc(s["topi_ok"], 1)
            dve.wait_ge(s["topi_ok"], 1)
            dve.tensor_copy(last[:, 0:1], topi[:, TOPK - 1:TOPK]).then_inc(s["lasti_ok"], 1)
            dve.wait_ge(s["lasti_ok"], 1)
            dve.wait_ge(s["consts_in"], 96)
            dve.tensor_scalar(keep[:, :], cnt[0:ROWS, 0:L], last[:, 0:1], None, ALU.is_le).then_inc(s["keep1_ok"], 1)
            dve.wait_ge(s["keep1_ok"], 1)
            dve.scalar_tensor_tensor(w_sb[:, :], corr[:, :], top[:, TOPK - 1:TOPK], keep[:, :], ALU.is_equal, ALU.mult).then_inc(s["keep2_ok"], 1)
            dve.wait_ge(s["keep2_ok"], 1)
            dve.scalar_tensor_tensor(keep[:, :], corr[:, :], top[:, TOPK - 1:TOPK], w_sb[:, :], ALU.is_gt, ALU.add).then_inc(s["keep3_ok"], 1)
            dve.wait_ge(s["keep3_ok"], 1)
            dve.wait_ge(s["exp_ok"], 1)
            dve.tensor_tensor_reduce(out=ex[:, :], in0=ex[:, :], in1=keep[:, :], scale=1.0, scalar=0.0,
                                     op0=ALU.mult, op1=ALU.add, accum_out=last[:, 2:3]).then_inc(s["wsum_ok"], 1)
            dve.wait_ge(s["wsum_ok"], 1)
            dve.reciprocal(last[:, 3:4], last[:, 2:3]).then_inc(s["wr_ok"], 1)
            dve.wait_ge(s["wr_ok"], 1)
            dve.tensor_scalar(w_sb[:, :], ex[:, :], last[:, 3:4], None, ALU.mult).then_inc(s["w_ok"], 1)
            dve.wait_ge(s["wt_done"], 1)
            dve.tensor_copy(wt[:, :, :], wt_ps[:, 0:S * ROWS].rearrange("p (s r) -> p s r", s=S)).then_inc(s["wt_ok"], 1)
            dve.wait_ge(s["wt_ok"], 1)
            dve.tensor_tensor(whalf[:, :, :], wt[:, 0:2], wt[:, 2:4], ALU.add).then_inc(s["whalf_ok"], 1)
            dve.tensor_tensor(wc[:, 2:4], wt[:, 0:2], wt[:, 2:4], ALU.subtract).then_inc(s["wc_ok"], 1)
            dve.wait_ge(s["whalf_ok"], 1)
            dve.tensor_tensor(wc[:, 0], whalf[:, 0], whalf[:, 1], ALU.add).then_inc(s["wc_ok"], 1)
            dve.tensor_tensor(wc[:, 1], whalf[:, 0], whalf[:, 1], ALU.subtract).then_inc(s["wc_ok"], 1)
            dve.wait_ge(s["gate_ok"], 2)
            falling = cnt[:, L:L + E]
            with nc.vector.Fori(0, B // 2) as i:
                for p in range(2):
                    b = i * 2 + p
                    wait(dve, "vp_ok", b - 2)
                    for c in range(C):
                        wait(dve, "wspec_done", b, c + 1)
                        wait(dve, "v_ok", b, c + 1)
                        products(p, c, wspec_ps[c], v_sb[:, b, c], "n_ok")
                    wait(dve, "even_done", b)
                    for n in range(2):
                        dve.scalar_tensor_tensor(x2_sb[:, p, 2 * n:2 * n + 2], even_ps[:, :].rearrange("p (s d) -> p s d", s=2), tg[:, 0:1],
                                                 x_sb[:, b, 2 * n:2 * n + 2], ALU.mult, ALU.add).then_inc(s["res1_ok"], 1)
                    wait(dve, "res1_ok", b)
                    wait(dve, "odd_done", b)
                    for n, k in ((0, 0), (1, 2)):
                        dve.scalar_tensor_tensor(x2_sb[:, p, 2 * n:2 * n + 2], odd_ps[:, :].rearrange("p (s d) -> p s d", s=2), tg[:, k:k + 1],
                                                 x2_sb[:, p, 2 * n:2 * n + 2], ALU.mult, ALU.add).then_inc(s["res2_ok"], 1)
                    wait(dve, "res2_ok", b)
                    statistics(lambda t: x2_sb[:, p, t], b, "stats2_ok", "aggr2_ok", "var2_ok", "rs2_ok", "newton2_ok")
                    for t in range(S):
                        dve.tensor_scalar(xn2[:, p, t], x2_sb[:, p, t], mv[:, t, 0:1], root[:, 3, t:t + 1],
                                          ALU.subtract, ALU.mult).then_inc(s["xn2_ok"], 1)
                    for t in range(S):
                        n, q = b * S + t, t % 2
                        wait(dve, "logit_done", n)
                        dve.tensor_copy(lg[:, q, 0], logit_ps).then_inc(s["lg_ok"], 1)
                        wait(dve, "lg_ok", n)
                        dve.tensor_reduce(col[:, q, 0:1], lg[:, q, 0], AX_X, ALU.max, negate=True).then_inc(s["nmax_ok"], 1)
                        wait(dve, "nmax_ok", n)
                        dve.tensor_scalar(lg[:, q, 2], lg[:, q, 0], col[:, q, 0:1], 0.0, ALU.add, ALU.is_equal).then_inc(s["first_ok"], 1)
                        wait(dve, "first_ok", n)
                        dve.tensor_tensor(lg[:, q, 3], lg[:, q, 2], falling, ALU.mult).then_inc(s["pick_ok"], 1)
                        wait(dve, "pick_ok", n)
                        dve.tensor_reduce(col[:, q, 2:3], lg[:, q, 3], AX_X, ALU.max).then_inc(s["big_ok"], 1)
                        wait(dve, "prob_ok", n)
                        dve.reciprocal(col[:, q, 3:4], col[:, q, 1:2]).then_inc(s["rden_ok"], 1)
                        wait(dve, "rden_ok", n)
                        dve.tensor_scalar(col[:, q, 4:5], col[:, q, 3:4], tg[:, 1:2], None, ALU.mult).then_inc(s["cw_ok"], 1)
                        wait(dve, "cw_ok", n)
                        wait(dve, "big_ok", n)
                        wait(dve, "ct_done", n - 2)
                        dve.tensor_scalar(c_sb[:, q], lg[:, q, 3], col[:, q, 2:3], col[:, q, 4:5], ALU.is_equal, ALU.mult).then_inc(s["c_ok"], 1)
                        wait(dve, "c_ok", n)
                        wait(dve, "ebias_done", n)
                        wait(dve, f"out_done{q}", i * S + (p * 2 + t // 2) - 1)
                        dve.tensor_tensor(acc[:, q], ebias_ps, x2_sb[:, p, t], ALU.add).then_inc(s["acc_ok"], 1)
                        wait(dve, "acc_ok", n)
                        for e in range(E):
                            if e % 2 == 0:
                                wait(dve, "expert_done", n, e // 2 + 1)
                            dve.scalar_tensor_tensor(acc[:, q], expert_ps[e // 2][:, e % 2 * D:e % 2 * D + D], c_sb[:, q, e:e + 1],
                                                     acc[:, q], ALU.mult, ALU.add).then_inc(s["sel_ok"], 1)
                            wait(dve, "sel_ok", n, e + 1)

        @block.tensor
        def _(pe):
            give_lead(pe, "tensor")
            matmul = nc.tensor.matmul

            def transform(ps, parts, done):
                matmul(ps[:, 0:P], parts(0), fwd[:, 0:P], start=True, stop=True)
                matmul(ps[:, P:2 * P], parts(1), fwd[:, P:2 * P], start=True, stop=True)
                matmul(ps[:, 2 * P:], parts(2), fwd[:, 2 * P:4 * P], start=True, stop=False)
                matmul(ps[:, 2 * P:], parts(3), fwd[:, 4 * P:6 * P], start=False, stop=True).then_inc(s[done], 1)

            def project(ps, w, n, m, spectrum, done):
                for c in range(C):
                    matmul(ps[:, :], w[:, c, m * P:(m + 1) * P], spectrum(c), start=(c == 0), stop=False)
                matmul(ps[:, 0:2], bias_sb[0:1, n, m * P:(m + 1) * P], crow[0:1, 0:2], start=False, stop=True).then_inc(s[done], 1)

            pe.wait_ge(s["table_in"], 16)
            with nc.tensor.Fori(0, B // 2) as i:
                for p in range(2):
                    b = i * 2 + p
                    wait(pe, "xc_ok", b)
                    for c in range(C):
                        wait(pe, "cf_ok", b - 1, c + 1)
                        transform(spectrum_ps[c], lambda k: xc[:, p, k, c * P:(c + 1) * P], "xspec_done")
                    wait(pe, "cc_ok", b)
                    for c in range(C):
                        wait(pe, "xf_ok", b, c + 1)
                        transform(spectrum_ps[c], lambda k: cc[:, p, k, c * P:(c + 1) * P], "cspec_done")
                    pe.wait_ge(s["w_in"], 32)
                    pe.wait_ge(s["row_in"], 80)
                    for m in range(C):
                        wait(pe, "m_ok", b - 1, 3 * m + 3)
                        project(q_ps[m], wq_sb, 0, m, lambda c: xf[:, p, c], "q_done")
                    wait(pe, "cf_ok", b)
                    for m in range(C):
                        wait(pe, "k_ok", b - 1, m + 1)
                        project(k_ps[m], wk_sb, 1, m, lambda c: cf[:, b, c], "k_done")
                    wait(pe, "prod_ok", b)
                    pe.wait_ge(s["consts_in"], 96)
                    for c in range(C):
                        for g in range(G):
                            mm = matmul(corr_spec_ps[:, bass.ds(b * H + (g * ROWS + c * HC), HC)],
                                        prod[:, p, c, g].rearrange("p r j -> p (r j)"), hones[:, :], start=True, stop=True)
                    mm.then_inc(s["sum_done"], 1)
            pe.wait_ge(s["cspec_ok"], 1)
            for g in range(G):
                mm = matmul(corr_ps[0:ROWS, :], corr_spec[:, g], inv[:, g], start=(g == 0), stop=(g == G - 1))
            mm.then_inc(s["corr_done"], 1)
            with nc.tensor.Fori(0, B) as b:
                for m in range(C):
                    wait(pe, "v_ok", b - 1, m + 1)
                    project(v_ps[m], wv_sb, 2, m, lambda c: cf[:, b, c], "v_done")
            pe.wait_ge(s["w_ok"], 1)
            for q in range(S):
                mm = nc.tensor.transpose(wt_ps[:, q * ROWS:(q + 1) * ROWS], w_sb[:, q * P:(q + 1) * P], idn[0:ROWS, 0:ROWS])
            mm.then_inc(s["wt_done"], 1)
            pe.wait_ge(s["wt_ok"], 1)
            wait(pe, "v_ok", B - 1)
            pe.wait_ge(s["late_in"], 64)
            with nc.tensor.Fori(0, B // 2) as i:
                for p in range(2):
                    b = i * 2 + p
                    wait(pe, "wstage_ok", b)
                    wait(pe, "res2_ok", b - 1)
                    for c in range(C):
                        transform(wspec_ps[c], lambda k: wstage[:, p, k, c * P:(c + 1) * P], "wspec_done")
                    wait(pe, "vp_ok", b)
                    wait(pe, "sel_ok", b * S - 1)
                    for h in range(2):
                        for g in (2 * h, 2 * h + 1):
                            ps = y_ps[h][:, g % 2 * D:g % 2 * D + D]
                            for c in range(C):
                                mm = matmul(ps, prod[:, p, c, g].rearrange("p r j -> p (r j)"), wo_sb[:, c],
                                            start=(c == 0), stop=(g > 0 and c == C - 1))
                            if g == 0:
                                mm = matmul(ps, crow[0:1, 0:P], bias_sb[0:1, 3], start=False, stop=True)
                        mm.then_inc(s["y_done"], 1)
                    wait(pe, "y_ok", b)
                    wait(pe, "n_ok", b)
                    for n in range(2):
                        for g in (0, 1):
                            mm = matmul(even_ps[:, n * D:(n + 1) * D], inv[:, g, n * P:(n + 1) * P], y_sb[:, p, g],
                                        start=(g == 0), stop=(g == 1))
                    mm.then_inc(s["even_done"], 1)
                    for n in range(2):
                        for g in (2, 3):
                            mm = matmul(odd_ps[:, n * D:(n + 1) * D], inv[:, g, n * P:(n + 1) * P], y_sb[:, p, g],
                                        start=(g == 2), stop=(g == 3))
                    mm.then_inc(s["odd_done"], 1)
                    for t in range(S):
                        n, q = b * S + t, t % 2
                        wait(pe, "xn2_ok", b, t + 1)
                        wait(pe, "xt_ok", n - 1)
                        for c in range(C):
                            mm = nc.tensor.transpose(turned_ps[:, c * P:(c + 1) * P], xn2[:, p, t, c * P:(c + 1) * P], idn[:, :])
                        mm.then_inc(s["turned_done"], 1)
                        wait(pe, "xt_ok", n)
                        wait(pe, "acc_ok", n - 1)
                        for c in range(C):
                            matmul(logit_ps, xt[:, q, c], rw_sb[:, c], start=(c == 0), stop=False)
                        matmul(logit_ps, crow[0:1, P:2 * P], rb_sb[0:1, :], start=False, stop=True).then_inc(s["logit_done"], 1)
                        for e in range(E // 2):
                            wait(pe, "sel_ok", n - 1, 2 * e + 2)
                            for c in range(C):
                                mm = matmul(expert_ps[e][:, :], xt[:, q, c], ew_sb[:, c, 2 * e:2 * e + 2], start=(c == 0), stop=(c == C - 1))
                            mm.then_inc(s["expert_done"], 1)
                        wait(pe, "c_ok", n)
                        nc.tensor.transpose(ct_ps, c_sb[:, q], idn[:, :]).then_inc(s["ct_done"], 1)
                        wait(pe, "ct_ok", n)
                        matmul(ebias_ps, ct[:, q], eb_sb[:, :], start=True, stop=True).then_inc(s["ebias_done"], 1)


_INS = ("x", "ctx", "g_xattn", "g_ffn", "wq", "wk", "wv", "wo", "bq", "bk", "bv", "bo", "rw", "rb", "ew", "eb",
        "fwd_table", "inv_table", "head_ones", "ident", "const_row", "counts")


def kernel(x, ctx_1024, g_xattn, g_ffn, L0_xattn_Wq, L0_xattn_bq, L0_xattn_Wk, L0_xattn_bk, L0_xattn_Wv, L0_xattn_bv,
           L0_xattn_Wo, L0_xattn_bo, L0_ffn_router_w, L0_ffn_router_b, L0_ffn_expert_w, L0_ffn_expert_b):
    import concourse.bacc as _bacc
    from concourse.bass_utils import run_bass_kernel_spmd as _run

    def turned(w):
        w = np.asarray(w)
        return w.T.reshape(C, P, w.shape[0]).transpose(1, 0, 2)

    row = lambda a: np.asarray(a).reshape(1, -1)
    fwd_table, inv_table = dft_tables()
    experts = np.asarray(L0_ffn_expert_w).transpose(2, 0, 1).reshape(C, P, E, D).transpose(1, 0, 2, 3)
    const_row = np.concatenate([[L], np.zeros(P - 1), np.ones(P)]).astype(np.float32)[None]
    counts = np.tile(np.concatenate([np.arange(L), np.arange(E, 0, -1)]).astype(np.float32), (P, 1))
    head_ones = (np.arange(P)[:, None] // DK == np.arange(HC)[None]).astype(np.float32)
    arrays = dict(zip(_INS, (
        x, ctx_1024, row(g_xattn), row(g_ffn), turned(L0_xattn_Wq), turned(L0_xattn_Wk), turned(L0_xattn_Wv), turned(L0_xattn_Wo),
        row(L0_xattn_bq), row(L0_xattn_bk), row(L0_xattn_bv), row(L0_xattn_bo), turned(L0_ffn_router_w), row(L0_ffn_router_b),
        experts, L0_ffn_expert_b, fwd_table, inv_table, head_ones, np.eye(P, dtype=np.float32), const_row, counts)))
    arrays = {n: np.ascontiguousarray(a) for n, a in arrays.items()}
    nc = _bacc.Bacc("TRN2", target_bir_lowering=False, num_devices=1)
    aps = {n: nc.dram_tensor(n + "_dram", a.shape, mybir.dt.from_np(a.dtype), kind="ExternalInput").ap() for n, a in arrays.items()}
    out = nc.dram_tensor("out_dram", (B, L, D), F32, kind="ExternalOutput").ap()
    build(nc, **aps, out=out)
    r = _run(nc, [{n + "_dram": a for n, a in arrays.items()}], core_ids=[0])
    return r.results[0]["out_dram"]
```

```python
from contextlib import ExitStack

import numpy as np

import concourse.bass as bass
from concourse import mybir

P = 128
B, L, D = 4, 512, 256
H, DK = 16, 16
E = 8
S = L // P
C = D // P
G = 4
J = 64
HC = P // DK
ROWS = B * H
PAIR = 2 * H
PAIRS = E // 2
RING = 3
TOPK = 6
EPS = 1e-5
F32 = mybir.dt.float32
F32R = mybir.dt.float32r
U32 = mybir.dt.uint32
ALU = mybir.AluOpType
ACT = mybir.ActivationFunctionType
AX_X = mybir.AxisListType.X
SMALL = dict(hones=HC, crow=P, idn=P, order=E, parts=2, rb=E, gates=2, bias=D, rw=C * E, eb=D)
PER_ROUND = dict(
    stats_ok=S, aggr_ok=S, var_ok=1, ln_ok=1, rs_ok=1, newton_ok=4, xn_ok=S, half_ok=1, xc_ok=3,
    chalf_ok=1, cc_ok=3, xspec_done=C, cspec_done=C, xhi_ok=C, xlo_ok=C, chi_ok=C, clo_ok=C,
    q_done=C, k_done=C, k_ok=C, m_ok=3 * C, prod0_ok=2, prod_ok=1, sum_done=1, v_done=C, v_ok=C,
    wspec_done=C, n_ok=3 * C, vp0_ok=2, vp_ok=1, y_done=2, y_ok=2, even_done=1, odd_done=1, res1_ok=2, res2_ok=2,
    stats2_ok=S, aggr2_ok=S, var2_ok=1, ln2_ok=1, rs2_ok=1, newton2_ok=4, xn2_ok=S,
    turned_done=C, thi_ok=C, tlo_ok=C, logit_done=1, lg0_ok=1, lg_ok=1, lmax_ok=1, shift_ok=1, prob_ok=1,
    psum_ok=1, rden_ok=1, first_ok=1, big_ok=1, cw_ok=1, c_ok=1, mask_ok=2, mt_done=1, mt_ok=1, ebias_done=S, bias_ok=S,
    expert_done=S * PAIRS, sel_ok=S * E, whole_ok=S, out0_done=16, out1_done=16, out2_done=16, out3_done=16,

    cspec_ok=1, corr_done=1, corr_ok=1, top_ok=1, topi_ok=1, lasti_ok=1, wmax_ok=1, exp_ok=1, keep1_ok=1, keep2_ok=1,
    keep3_ok=1, wsum_ok=1, wr_ok=1, w_ok=1, wt_done=1, wt_ok=1, whalf_ok=1, wc_ok=3, wf_done=1, wfhi_ok=1, wflo_ok=1)
ONCE = """table_in small_in wqk_in wvo_in inv_in cnt_in pick_in ew_in gate_ok whi_ok wlo_ok pick_ok
    ewhi_ok ewlo_ok rwhi_ok rwlo_ok ebhi_ok eblo_ok ebpart_ok eb_ok zero_ok""".split()


def after(name, r, k=None):
    n = PER_ROUND[name]
    return r * n + (n if k is None else k)


def dft_tables():
    t = np.arange(L)
    j = np.arange(J)
    f = [4 * j, 4 * j + 2, 4 * j + 1, 4 * j + 3]

    def angle(times, freqs):
        return 2 * np.pi * ((times[:, None] * freqs[None, :]) % L) / L

    q = t[:P]
    forward = []
    for g in (0, 1):
        a = angle(q, f[g])
        re, im = np.cos(a), -np.sin(a)
        if g == 0:
            im[:, 0] = np.where(q % 2 == 0, 1.0, -1.0)
        forward += [re, im]
    for g in (2, 3):
        a = angle(q, f[g])
        forward += [np.cos(a), -np.sin(a)]
    for g, sign in ((2, -1.0), (3, 1.0)):
        a = angle(q, f[g])
        forward += [sign * np.sin(a), sign * np.cos(a)]
    inverse = np.zeros((2, J, G, L))
    for g in range(G):
        a = angle(t, f[g]).T
        inverse[0, :, g] = 2.0 * np.cos(a) / L
        inverse[1, :, g] = -2.0 * np.sin(a) / L
    inverse[0, 0, 0] = 1.0 / L
    inverse[1, 0, 0] = np.where(t % 2 == 0, 1.0, -1.0) / L
    return (np.concatenate(forward, 1).astype(np.float32),
            inverse.reshape(P, G * L).astype(np.float32))


def build(nc, x, ctx, wqk, wvo, ew, fwd_table, inv_table, small_in, counts, head_pick, out):
    es = ExitStack()
    with es:
        def sb(name, shape, dt=F32):
            return es.enter_context(nc.sbuf_tensor(name, shape, dt))

        bank = [es.enter_context(nc.psum_tensor(f"bank{n}", [P, 512], F32)) for n in range(8)]
        x_spec_ps = bank[0:2]
        c_spec_ps = [bank[2:4], bank[4:6], bank[0:2], bank[0:2]]
        q_ps = bank[2:4]
        k_ps = v_ps = bank[4:6]
        corr_spec_ps = bank[6]
        corr_ps = bank[7]
        wt_ps = bank[7]
        wf_ps = bank[7]
        wspec_ps = bank[0:2]
        y_ps = [bank[2:4], bank[4:6], bank[2:4], bank[2:4]]
        even_ps = [bank[n] for n in (2, 0, 2, 2)]
        odd_ps = [bank[n] for n in (3, 1, 3, 3)]
        turned_ps = bank[2:4]
        expert_ps = bank[4:4 + RING]
        logit_ps = bank[7][:, 0:S * 2 * E]
        mt_ps = bank[7][:, P:2 * P]
        ebias_ps = bank[7][:, 2 * P:2 * P + D]

        fwd = sb("fwd", [P, 6 * P])
        inv = sb("inv", [P, G, L])
        small = sb("small", [P, sum(SMALL.values())])
        part = {}
        for name, width in SMALL.items():
            start = sum(w for n, w in SMALL.items() if n in part)
            part[name] = small[:, start:start + width]
        hones = part["hones"]
        crow = part["crow"]
        idn = part["idn"]
        order = part["order"]
        parts = part["parts"]
        bias = part["bias"]
        gates = part["gates"]
        rb_sb = part["rb"]
        rw_raw = part["rw"].rearrange("p (c e) -> p c e", c=C)
        eb_raw = part["eb"]
        pick = sb("pick", [PAIR, 2, C, P], F32R)
        w_raw = sb("w_raw", [P, 4, C, D])
        w_hi = sb("w_hi", [P, 3, C, D], F32R)
        w_lo = sb("w_lo", [P, 3, C, D], F32R)
        rw_sb = sb("rw_sb", [P, C, 2, E], F32R)
        ew_raw = sb("ew_raw", [P, C * PAIRS, 2 * D])
        ew_hi = sb("ew_hi", [P, C * PAIRS, 2 * D], F32R)
        ew_lo = sb("ew_lo", [P, C * PAIRS, 2 * D], F32R)
        eb_sb = sb("eb_sb", [P, D], F32R)
        tg = sb("tg", [P, 3])

        x_sb = sb("x_sb", [P, B, S, D])
        ctx_sb = sb("ctx_sb", [P, 2, S, D])
        stats = sb("stats", [P, S, 6])
        mv = sb("mv", [P, S, 2])
        root = sb("root", [P, 5, S])
        xn = sb("xn", [P, S, D])
        half = sb("half", [P, 2, D])
        chalf = sb("chalf", [P, 2, D])
        xc = sb("xc", [P, 2, 4, D])
        cc = sb("cc", [P, 2, 4, D])
        x_hi = sb("x_hi", [P, 2, C, L], F32R)
        x_lo = sb("x_lo", [P, 2, C, L], F32R)
        c_hi = sb("c_hi", [P, B, C, L], F32R)
        c_lo = sb("c_lo", [P, B, C, L], F32R)
        k_sb = sb("k_sb", [P, C, L])
        m1 = sb("m1", [P, C, G, 2, J])
        m2 = sb("m2", [P, C, G, 2, J])
        prod = sb("prod", [P, 2, C, G, 2, J])
        v_sb = ew_raw[:, :, :].rearrange("p (b c) l -> p b c l", b=B)
        corr_spec = xn[:, 0, 0:G * PAIR].rearrange("p (g r) -> p g r", g=G)
        corr = xn[0:PAIR, 0:2].rearrange("p a d -> p (a d)")
        ex = xn[0:PAIR, 2:4].rearrange("p a d -> p (a d)")
        keep = half[0:PAIR, :, :].rearrange("p a d -> p (a d)")
        w_sb = chalf[0:PAIR, :, :].rearrange("p a d -> p (a d)")
        top = sb("top", [PAIR, 8])
        topi = sb("topi", [PAIR, 8], U32)
        last = sb("last", [PAIR, 4])
        wt = w_raw[:, 2, 1, 0:S * PAIR].rearrange("p (s r) -> p s r", s=S)
        whalf = half[:, 0, 0:2 * PAIR].rearrange("p (s r) -> p s r", s=2)
        wc = chalf[:, 0, 0:4 * PAIR].rearrange("p (k r) -> p k r", k=4)
        wf_hi = sb("wf_hi", [PAIR, L], F32R)
        wf_lo = sb("wf_lo", [PAIR, L], F32R)
        cnt = w_raw[0:PAIR, 1].rearrange("p c d -> p (c d)")
        pick_raw = w_raw[0:PAIR, 0].rearrange("p c d -> p (c d)")
        eb_lo = w_raw[:, 2, 0]

        y_sb = cc
        x2_sb = ctx_sb
        xn2 = xc
        t_hi, t_lo = c_hi, c_lo
        lg = sb("lg", [P, 4, S, E])
        col = sb("col", [P, 4, S])
        cw = sb("cw", [P, 2, S])
        c_sb = sb("c_sb", [P, 2, S, E])
        mask = sb("mask", [P, S, 32])
        mt = sb("mt", [P, P], F32R)
        acc = w_raw[:, 0:2].rearrange("p a c d -> p (a c) d")
        gated = xn

        s = {n: es.enter_context(nc.semaphore(n)) for n in (*PER_ROUND, *ONCE)}
        x_in = [es.enter_context(nc.semaphore(f"x_in{b}")) for b in range(B)]
        c_in = [es.enter_context(nc.semaphore(f"c_in{b}")) for b in range(B)]
        block = es.enter_context(nc.Block())

        def wait(eng, name, r, k=None):
            if after(name, r, k) > 0:
                eng.wait_ge(s[name], after(name, r, k))

        def f32(t):
            return t.bitcast(F32)

        @block.sync
        def _(sp):
            def load_x(b):
                sp.dma_start(x_sb[:, b], x[b].rearrange("(s p) d -> p s d", p=P)).then_inc(x_in[b], 16)

            def load_context(b):
                wait(sp, "cc_ok", b - 2)
                sp.dma_start(ctx_sb[:, b % 2], ctx[b].rearrange("(s p) d -> p s d", p=P)).then_inc(c_in[b], 16)

            load_x(0)
            load_context(0)
            sp.dma_start(fwd[:, :], fwd_table).then_inc(s["table_in"], 16)
            load_x(1)
            sp.dma_start(w_raw[:, 0:2], wqk).then_inc(s["wqk_in"], 16)
            sp.dma_start(small[:, :], small_in).then_inc(s["small_in"], 16)
            load_context(1)
            sp.dma_start(w_raw[:, 2:4], wvo).then_inc(s["wvo_in"], 16)
            load_x(2)
            sp.dma_start(ew_raw[:, :, :], ew).then_inc(s["ew_in"], 16)
            load_context(2)
            load_x(3)
            sp.dma_start(inv[:, :, :], inv_table.rearrange("p (g t) -> p g t", g=G)).then_inc(s["inv_in"], 16)
            load_context(3)
            sp.wait_ge(s["wlo_ok"], 1)
            sp.dma_start(pick_raw, head_pick).then_inc(s["pick_in"], 16)
            sp.wait_ge(s["wlo_ok"], 2)
            sp.dma_start(cnt, counts).then_inc(s["cnt_in"], 16)
            for b in range(B):
                for t in range(S):
                    wait(sp, "whole_ok", b, t + 1)
                    sp.dma_start(out[b, t * P:(t + 1) * P, :], acc[:, t]).then_inc(s[f"out{t}_done"], 16)
            for t in range(S):
                wait(sp, f"out{t}_done", B - 1)

        @block.gpsimd
        def _(pool):
            def context(b):
                p = b % 2
                pool.wait_ge(c_in[b], 16)
                wait(pool, "cspec_done", b - 2)
                pool.tensor_tensor(cc[:, p, 2:4], ctx_sb[:, p, 0:2], ctx_sb[:, p, 2:4], ALU.subtract).then_inc(s["cc_ok"], 1)
                pool.tensor_tensor(chalf[:, :, :], ctx_sb[:, p, 0:2], ctx_sb[:, p, 2:4], ALU.add).then_inc(s["chalf_ok"], 1)
                wait(pool, "chalf_ok", b)
                pool.tensor_tensor(cc[:, p, 0], chalf[:, 0], chalf[:, 1], ALU.add).then_inc(s["cc_ok"], 1)
                pool.tensor_tensor(cc[:, p, 1], chalf[:, 0], chalf[:, 1], ALU.subtract).then_inc(s["cc_ok"], 1)
                wait(pool, "cc_ok", b)

            def weights_low(n):
                pool.wait_ge(s["whi_ok"], n + 1)
                pool.tensor_tensor(w_lo[:, n], w_raw[:, n], f32(w_hi[:, n]), ALU.subtract).then_inc(s["wlo_ok"], 1)

            def combine(b, made, mid, done, op_re, op_im):
                p = b % 2
                wait(pool, made, b)
                a = m1[:, :, :, :, :].rearrange("p c g r j -> p (c g) r j")
                m = m2[:, :, :, :, :].rearrange("p c g r j -> p (c g) r j")
                o = prod[:, p].rearrange("p c g r j -> p (c g) r j")
                pool.tensor_tensor(o[:, :, 0], a[:, :, 0], a[:, :, 1], op_re).then_inc(s[mid], 1)
                pool.tensor_tensor(o[:, :, 1], m[:, :, 1], m[:, :, 0], op_im).then_inc(s[mid], 1)
                wait(pool, mid, b)
                pool.tensor_copy(prod[:, p, :, 0, :, 0], m1[:, :, 0, :, 0]).then_inc(s[done], 1)

            def correlate(b):
                wait(pool, "sum_done", b - 2)
                combine(b, "m_ok", "prod0_ok", "prod_ok", ALU.add, ALU.subtract)

            def convolve(b):
                if b < 2:
                    wait(pool, "sum_done", b + 2)
                else:
                    wait(pool, "y_done", b - 2)
                combine(b, "n_ok", "vp0_ok", "vp_ok", ALU.subtract, ALU.add)

            def finish(b, tiles):
                for t in tiles:
                    wait(pool, "bias_ok", b, t + 1)
                    wait(pool, "sel_ok", b, (t + 1) * E)
                    pool.tensor_tensor(acc[:, t], acc[:, t], gated[:, t], ALU.add).then_inc(s["whole_ok"], 1)

            context(0)
            weights_low(0)
            weights_low(1)
            context(1)
            pool.memset(mask[:, :, :], 0.0).then_inc(s["zero_ok"], 1)
            weights_low(2)
            context(2)
            context(3)
            for b in range(B):
                correlate(b)
            convolve(0)
            convolve(1)
            for b in range(B):
                if b + 2 < B:
                    convolve(b + 2)
                finish(b, range(S))

        @block.scalar
        def _(act):
            act.preload_act_table_set("natural_log_exp_and_others")

            def log_root(b, var_ok, ln_ok, rs_ok):
                wait(act, var_ok, b)
                act.activation(root[:, 1], root[:, 0], ACT.Ln).then_inc(s[ln_ok], 1)
                wait(act, ln_ok, b)
                act.activation(root[:, 2], root[:, 1], ACT.Exp, scale=-0.5).then_inc(s[rs_ok], 1)

            def normalise(dst, src, done):
                for t in range(S):
                    act.activation(dst(t), src(t), ACT.Identity, bias=root[:, 4, t:t + 1], scale=root[:, 3, t:t + 1]).then_inc(s[done], 1)

            def normalise_x(b):
                wait(act, "newton_ok", b)
                wait(act, "xc_ok", b - 1)
                normalise(lambda t: xn[:, t], lambda t: x_sb[:, b, t], "xn_ok")

            def normalise_tokens(b):
                wait(act, "newton2_ok", b)
                wait(act, "turned_done", b - 2)
                normalise(lambda t: xn2[:, b % 2, t], lambda t: x2_sb[:, b % 2, t], "xn2_ok")

            def split_weight(n):
                act.copy(w_hi[:, n], w_raw[:, n]).then_inc(s["whi_ok"], 1)

            def split_experts(ks):
                for k in ks:
                    act.copy(ew_hi[:, k], ew_raw[:, k]).then_inc(s["ewhi_ok"], 1)

            def x_spectrum(b):
                wait(act, "q_done", b - 2)
                for c in range(C):
                    wait(act, "xspec_done", b, c + 1)
                    act.copy(x_hi[:, b % 2, c], x_spec_ps[c][:, :]).then_inc(s["xhi_ok"], 1)

            def c_spectrum(b):
                for c in range(C):
                    wait(act, "cspec_done", b, c + 1)
                    act.copy(c_hi[:, b, c], c_spec_ps[b][c][:, :]).then_inc(s["chi_ok"], 1)

            def k_out(b):
                wait(act, "m_ok", b - 1)
                for c in range(C):
                    wait(act, "k_done", b, c + 1)
                    act.copy(k_sb[:, c], k_ps[c][:, :]).then_inc(s["k_ok"], 1)

            def v_out(b):
                for c in range(C):
                    wait(act, "v_done", b, c + 1)
                    act.copy(v_sb[:, b, c], v_ps[c][:, :]).then_inc(s["v_ok"], 1)

            def exponentials(r):
                wait(act, "top_ok", r)
                act.mul(last[:, 1:2], top[:, 0:1], -1.0 / DK).then_inc(s["wmax_ok"], 1)
                wait(act, "wmax_ok", r)
                act.activation(ex, corr, ACT.Exp, bias=last[:, 1:2], scale=1.0 / DK).then_inc(s["exp_ok"], 1)

            def weights_out(r):
                wait(act, "wf_done", r)
                wait(act, "wspec_done", 2 * r - 1)
                act.copy(wf_hi[:, :], wf_ps[0:PAIR, :]).then_inc(s["wfhi_ok"], 1)

            def y_out(b):
                wait(act, "odd_done", b - 2)
                for h in range(2):
                    wait(act, "y_done", b, h + 1)
                    act.copy(y_sb[:, b % 2, 2 * h:2 * h + 2], y_ps[b][h][:, :].rearrange("p (g d) -> p g d", g=2)).then_inc(s["y_ok"], 1)

            def tokens_out(b):
                for c in range(C):
                    wait(act, "turned_done", b, c + 1)
                    act.copy(t_hi[:, b, c], turned_ps[c][:, :]).then_inc(s["thi_ok"], 1)

            def router(b):
                wait(act, "shift_ok", b)
                act.activation(lg[:, 2], lg[:, 1], ACT.Exp).then_inc(s["prob_ok"], 1)

            def masks_out(b):
                wait(act, "mt_done", b)
                wait(act, "ebias_done", b - 1)
                act.copy(mt[:, :], mt_ps).then_inc(s["mt_ok"], 1)

            def bias_out(b, t):
                wait(act, "ebias_done", b, t + 1)
                wait(act, "cw_ok", b)
                wait(act, "whole_ok", b - 1, t + 1)
                act.mul(gated[:, t], ebias_ps, cw[:, b % 2, t:t + 1]).then_inc(s["bias_ok"], 1)

            log_root(0, "var_ok", "ln_ok", "rs_ok")
            normalise_x(0)
            log_root(1, "var_ok", "ln_ok", "rs_ok")
            act.wait_ge(s["wqk_in"], 16)
            split_weight(0)
            split_weight(1)
            normalise_x(1)
            x_spectrum(0)
            log_root(2, "var_ok", "ln_ok", "rs_ok")
            c_spectrum(0)
            normalise_x(2)
            x_spectrum(1)
            c_spectrum(1)
            act.wait_ge(s["wvo_in"], 16)
            split_weight(2)
            act.wait_ge(s["ew_in"], 16)
            split_experts(range(0, 2))
            k_out(0)
            log_root(3, "var_ok", "ln_ok", "rs_ok")
            x_spectrum(2)
            normalise_x(3)
            c_spectrum(2)
            split_experts(range(2, 4))
            k_out(1)
            split_experts(range(4, C * PAIRS))
            x_spectrum(3)
            c_spectrum(3)
            act.wait_ge(s["pick_in"], 16)
            act.copy(pick[:, :, :, :], pick_raw.rearrange("p (b c d) -> p b c d", b=2, c=C)).then_inc(s["pick_ok"], 1)
            act.wait_ge(s["small_in"], 16)
            act.copy(rw_sb[:, :, 0], rw_raw).then_inc(s["rwhi_ok"], 1)
            act.copy(eb_sb[:, :], eb_raw).then_inc(s["ebhi_ok"], 1)
            v_out(0)
            exponentials(0)
            k_out(2)
            v_out(1)
            k_out(3)
            weights_out(0)
            act.activation(tg[:, 0:2], gates, ACT.Tanh).then_inc(s["gate_ok"], 1)
            act.wait_ge(s["gate_ok"], 1)
            act.mul(tg[:, 2:3], tg[:, 0:1], -1.0).then_inc(s["gate_ok"], 1)
            act.preload_act_table_set("natural_log_exp_and_others")
            v_out(2)
            exponentials(1)
            y_out(0)
            v_out(3)
            log_root(0, "var2_ok", "ln2_ok", "rs2_ok")
            weights_out(1)
            normalise_tokens(0)
            y_out(1)
            tokens_out(0)
            router(0)
            for b in range(B):
                masks_out(b)
                if 1 <= b and b + 1 < B:
                    y_out(b + 1)
                for t in range(3):
                    bias_out(b, t)
                if b + 1 < B:
                    log_root(b + 1, "var2_ok", "ln2_ok", "rs2_ok")
                bias_out(b, 3)
                if b + 1 < B:
                    normalise_tokens(b + 1)
                    tokens_out(b + 1)
                    router(b + 1)

        @block.vector
        def _(dve):
            def variances(src, b, stats_ok, aggr_ok, var_ok):
                for t in range(S):
                    dve.bn_stats(stats[:, t], src(t)).then_inc(s[stats_ok], 1)
                wait(dve, stats_ok, b)
                for t in range(S):
                    dve.bn_aggr(mv[:, t], stats[:, t]).then_inc(s[aggr_ok], 1)
                wait(dve, aggr_ok, b)
                dve.tensor_scalar(root[:, 0], mv[:, :, 1], EPS, None, ALU.add).then_inc(s[var_ok], 1)

            def roots(b, rs_ok, newton_ok):
                wait(dve, rs_ok, b)
                dve.scalar_tensor_tensor(root[:, 1], root[:, 2], -0.5, root[:, 2], ALU.mult, ALU.mult).then_inc(s[newton_ok], 1)
                wait(dve, newton_ok, b, 1)
                dve.tensor_tensor(root[:, 1], root[:, 1], root[:, 0], ALU.mult).then_inc(s[newton_ok], 1)
                wait(dve, newton_ok, b, 2)
                dve.scalar_tensor_tensor(root[:, 3], root[:, 1], 1.5, root[:, 2], ALU.add, ALU.mult).then_inc(s[newton_ok], 1)
                wait(dve, newton_ok, b, 3)
                dve.scalar_tensor_tensor(root[:, 4], mv[:, :, 0], -1.0, root[:, 3], ALU.mult, ALU.mult).then_inc(s[newton_ok], 1)

            def x_statistics(b):
                dve.wait_ge(x_in[b], 16)
                wait(dve, "xn_ok", b - 1)
                variances(lambda t: x_sb[:, b, t], b, "stats_ok", "aggr_ok", "var_ok")

            def x_roots(b):
                roots(b, "rs_ok", "newton_ok")

            def x_combinations(b):
                p = b % 2
                wait(dve, "xspec_done", b - 2)
                wait(dve, "xn_ok", b)
                dve.tensor_tensor(half[:, :, :], xn[:, 0:2], xn[:, 2:4], ALU.add).then_inc(s["half_ok"], 1)
                dve.tensor_tensor(xc[:, p, 2:4], xn[:, 0:2], xn[:, 2:4], ALU.subtract).then_inc(s["xc_ok"], 1)
                wait(dve, "half_ok", b)
                dve.tensor_tensor(xc[:, p, 0], half[:, 0], half[:, 1], ALU.add).then_inc(s["xc_ok"], 1)
                dve.tensor_tensor(xc[:, p, 1], half[:, 0], half[:, 1], ALU.subtract).then_inc(s["xc_ok"], 1)
                wait(dve, "xc_ok", b)

            def x_low(b):
                for c in range(C):
                    wait(dve, "xhi_ok", b, c + 1)
                    dve.tensor_tensor(x_lo[:, b % 2, c], x_spec_ps[c][:, :], f32(x_hi[:, b % 2, c]), ALU.subtract).then_inc(s["xlo_ok"], 1)

            def c_low(b):
                for c in range(C):
                    wait(dve, "chi_ok", b, c + 1)
                    dve.tensor_tensor(c_lo[:, b, c], c_spec_ps[b][c][:, :], f32(c_hi[:, b, c]), ALU.subtract).then_inc(s["clo_ok"], 1)

            def tokens_low(b):
                for c in range(C):
                    wait(dve, "thi_ok", b, c + 1)
                    dve.tensor_tensor(t_lo[:, b, c], turned_ps[c][:, :], f32(t_hi[:, b, c]), ALU.subtract).then_inc(s["tlo_ok"], 1)

            def products(c, a_ps, k, done):
                a = a_ps[:, :].rearrange("p (g r j) -> p g r j", g=G, r=2)
                k = k.rearrange("p (g r j) -> p g r j", g=G, r=2)
                dve.tensor_tensor(m1[:, c], a, k, ALU.mult).then_inc(s[done], 1)
                dve.tensor_tensor(m2[:, c, :, 0], a[:, :, 0], k[:, :, 1], ALU.mult).then_inc(s[done], 1)
                dve.tensor_tensor(m2[:, c, :, 1], a[:, :, 1], k[:, :, 0], ALU.mult).then_inc(s[done], 1)

            def correlate(b):
                wait(dve, "prod_ok", b - 1)
                for c in range(C):
                    wait(dve, "k_ok", b, c + 1)
                    wait(dve, "q_done", b, c + 1)
                    products(c, q_ps[c], k_sb[:, c], "m_ok")

            def convolve(b):
                wait(dve, "prod_ok", B - 1)
                wait(dve, "vp_ok", b - 1)
                for c in range(C):
                    wait(dve, "wspec_done", b, c + 1)
                    wait(dve, "v_ok", b, c + 1)
                    products(c, wspec_ps[c], v_sb[:, b, c], "n_ok")

            def split_experts(ks):
                for k in ks:
                    dve.wait_ge(s["ewhi_ok"], k + 1)
                    dve.tensor_tensor(ew_lo[:, k], ew_raw[:, k], f32(ew_hi[:, k]), ALU.subtract).then_inc(s["ewlo_ok"], 1)

            def correlation_spectra(r):
                wait(dve, "sum_done", 2 * r + 1)
                wait(dve, "w_ok", r - 1)
                dve.tensor_copy(corr_spec, corr_spec_ps[:, 0:G * ROWS].rearrange("p (g r) -> p g r", g=G)
                                [:, :, r * PAIR:(r + 1) * PAIR]).then_inc(s["cspec_ok"], 1)

            def rank(r):
                wait(dve, "corr_done", r)
                dve.tensor_copy(corr, corr_ps[0:PAIR, :]).then_inc(s["corr_ok"], 1)
                wait(dve, "corr_ok", r)
                dve.max(top[:, :], corr).then_inc(s["top_ok"], 1)
                wait(dve, "top_ok", r)
                dve.max_index(topi[:, :], top[:, :], corr).then_inc(s["topi_ok"], 1)
                wait(dve, "topi_ok", r)
                dve.tensor_copy(last[:, 0:1], topi[:, TOPK - 1:TOPK]).then_inc(s["lasti_ok"], 1)
                wait(dve, "lasti_ok", r)
                dve.wait_ge(s["cnt_in"], 16)
                dve.tensor_scalar(keep, cnt, last[:, 0:1], None, ALU.is_le).then_inc(s["keep1_ok"], 1)
                wait(dve, "keep1_ok", r)
                wait(dve, "wf_done", r - 1)
                dve.scalar_tensor_tensor(w_sb, corr, top[:, TOPK - 1:TOPK], keep, ALU.is_equal, ALU.mult).then_inc(s["keep2_ok"], 1)
                wait(dve, "keep2_ok", r)
                dve.scalar_tensor_tensor(keep, corr, top[:, TOPK - 1:TOPK], w_sb, ALU.is_gt, ALU.add).then_inc(s["keep3_ok"], 1)
                wait(dve, "keep3_ok", r)
                wait(dve, "exp_ok", r)
                dve.tensor_tensor_reduce(out=ex, in0=ex, in1=keep, scale=1.0, scalar=0.0,
                                         op0=ALU.mult, op1=ALU.add, accum_out=last[:, 2:3]).then_inc(s["wsum_ok"], 1)
                wait(dve, "wsum_ok", r)
                dve.reciprocal(last[:, 3:4], last[:, 2:3]).then_inc(s["wr_ok"], 1)
                wait(dve, "wr_ok", r)
                dve.tensor_scalar(w_sb, ex, last[:, 3:4], None, ALU.mult).then_inc(s["w_ok"], 1)

            def weight_combinations(r):
                wait(dve, "wt_done", r)
                dve.tensor_copy(wt, wt_ps[:, 0:S * PAIR].rearrange("p (s r) -> p s r", s=S)).then_inc(s["wt_ok"], 1)
                wait(dve, "wt_ok", r)
                dve.tensor_tensor(whalf, wt[:, 0:2], wt[:, 2:4], ALU.add).then_inc(s["whalf_ok"], 1)
                dve.tensor_tensor(wc[:, 2:4], wt[:, 0:2], wt[:, 2:4], ALU.subtract).then_inc(s["wc_ok"], 1)
                wait(dve, "whalf_ok", r)
                dve.tensor_tensor(wc[:, 0], whalf[:, 0], whalf[:, 1], ALU.add).then_inc(s["wc_ok"], 1)
                dve.tensor_tensor(wc[:, 1], whalf[:, 0], whalf[:, 1], ALU.subtract).then_inc(s["wc_ok"], 1)
                wait(dve, "wc_ok", r)

            def weights_low(r):
                wait(dve, "wfhi_ok", r)
                wait(dve, "wspec_done", 2 * r - 1)
                dve.tensor_tensor(wf_lo[:, :], wf_ps[0:PAIR, :], f32(wf_hi[:, :]), ALU.subtract).then_inc(s["wflo_ok"], 1)

            def split_small():
                dve.wait_ge(s["rwhi_ok"], 1)
                dve.tensor_tensor(rw_sb[:, :, 1], rw_raw, f32(rw_sb[:, :, 0]), ALU.subtract).then_inc(s["rwlo_ok"], 1)
                dve.wait_ge(s["ebhi_ok"], 1)
                dve.tensor_tensor(eb_lo, eb_raw, f32(eb_sb[:, :]), ALU.subtract).then_inc(s["eblo_ok"], 1)
                dve.wait_ge(s["eblo_ok"], 1)
                dve.tensor_scalar(eb_lo, eb_lo, parts[:, 1:2], None, ALU.mult).then_inc(s["ebpart_ok"], 1)
                dve.wait_ge(s["ebpart_ok"], 1)
                dve.scalar_tensor_tensor(eb_sb[:, :], f32(eb_sb[:, :]), parts[:, 0:1], eb_lo, ALU.mult, ALU.add).then_inc(s["eb_ok"], 1)

            def residual(b):
                p = b % 2
                wait(dve, "even_done", b)
                dve.wait_ge(s["gate_ok"], 2)
                for n in range(2):
                    dve.scalar_tensor_tensor(x2_sb[:, p, 2 * n:2 * n + 2], even_ps[b][:, :].rearrange("p (s d) -> p s d", s=2), tg[:, 0:1],
                                             x_sb[:, b, 2 * n:2 * n + 2], ALU.mult, ALU.add).then_inc(s["res1_ok"], 1)
                wait(dve, "res1_ok", b)
                wait(dve, "odd_done", b)
                for n, k in ((0, 0), (1, 2)):
                    dve.scalar_tensor_tensor(x2_sb[:, p, 2 * n:2 * n + 2], odd_ps[b][:, :].rearrange("p (s d) -> p s d", s=2), tg[:, k:k + 1],
                                             x2_sb[:, p, 2 * n:2 * n + 2], ALU.mult, ALU.add).then_inc(s["res2_ok"], 1)

            def token_variances(b):
                wait(dve, "res2_ok", b)
                wait(dve, "xn2_ok", b - 1)
                variances(lambda t: x2_sb[:, b % 2, t], b, "stats2_ok", "aggr2_ok", "var2_ok")

            def router(b):
                p = b % 2

                def wide(t):
                    return t.unsqueeze(2).to_broadcast([P, S, E])

                logits = logit_ps.rearrange("p (s k e) -> p s k e", s=S, k=2)
                wait(dve, "logit_done", b)
                dve.tensor_tensor(lg[:, 0], logits[:, :, 0], rb_sb.unsqueeze(1).to_broadcast([P, S, E]), ALU.add).then_inc(s["lg0_ok"], 1)
                wait(dve, "lg0_ok", b)
                dve.tensor_tensor(lg[:, 0], logits[:, :, 1], lg[:, 0], ALU.add).then_inc(s["lg_ok"], 1)
                wait(dve, "lg_ok", b)
                dve.tensor_reduce(col[:, 0], lg[:, 0], AX_X, ALU.max).then_inc(s["lmax_ok"], 1)
                wait(dve, "lmax_ok", b)
                dve.tensor_tensor(lg[:, 1], lg[:, 0], wide(col[:, 0]), ALU.subtract).then_inc(s["shift_ok"], 1)
                wait(dve, "shift_ok", b)
                dve.scalar_tensor_tensor(lg[:, 3], lg[:, 1], 0.0, order.unsqueeze(1).to_broadcast([P, S, E]),
                                         ALU.is_equal, ALU.mult).then_inc(s["first_ok"], 1)
                wait(dve, "first_ok", b)
                dve.tensor_reduce(col[:, 3], lg[:, 3], AX_X, ALU.max).then_inc(s["big_ok"], 1)
                wait(dve, "big_ok", b)
                dve.wait_ge(s["zero_ok"], 1)
                wait(dve, "mt_done", b - 1)
                for k in range(2):
                    dve.tensor_tensor(mask[:, :, k * E:(k + 1) * E], lg[:, 3], wide(col[:, 3]), ALU.is_equal).then_inc(s["mask_ok"], 1)
                wait(dve, "prob_ok", b)
                dve.tensor_reduce(col[:, 1], lg[:, 2], AX_X, ALU.add).then_inc(s["psum_ok"], 1)
                wait(dve, "psum_ok", b)
                dve.reciprocal(col[:, 2], col[:, 1]).then_inc(s["rden_ok"], 1)
                wait(dve, "rden_ok", b)
                wait(dve, "bias_ok", b - 2)
                dve.tensor_scalar(cw[:, p], col[:, 2], tg[:, 1:2], None, ALU.mult).then_inc(s["cw_ok"], 1)
                wait(dve, "cw_ok", b)
                dve.tensor_tensor(c_sb[:, p], mask[:, :, 0:E], wide(cw[:, p]), ALU.mult).then_inc(s["c_ok"], 1)
                wait(dve, "c_ok", b)

            def select(b, t, pairs):
                for n in pairs:
                    wait(dve, "expert_done", b, t * PAIRS + n + 1)
                    if n == 0:
                        wait(dve, f"out{t}_done", b - 1)
                    for e in (2 * n, 2 * n + 1):
                        if e:
                            wait(dve, "sel_ok", b, t * E + e)
                        ps = expert_ps[((b * S + t) * PAIRS + n) % RING]
                        dve.scalar_tensor_tensor(acc[:, t], ps[:, e % 2 * D:e % 2 * D + D], c_sb[:, b % 2, t, e:e + 1],
                                                 acc[:, t] if e else x2_sb[:, b % 2, t], ALU.mult, ALU.add).then_inc(s["sel_ok"], 1)

            x_statistics(0)
            x_roots(0)
            x_combinations(0)
            x_statistics(1)
            x_roots(1)
            x_combinations(1)
            x_low(0)
            x_statistics(2)
            c_low(0)
            x_roots(2)
            x_low(1)
            x_combinations(2)
            c_low(1)
            x_statistics(3)
            correlate(0)
            x_roots(3)
            split_experts(range(0, 2))
            x_low(2)
            x_combinations(3)
            c_low(2)
            split_experts(range(2, 4))
            correlate(1)
            split_experts(range(4, C * PAIRS))
            x_low(3)
            c_low(3)
            correlation_spectra(0)
            rank(0)
            correlate(2)
            weight_combinations(0)
            split_small()
            correlate(3)
            weights_low(0)
            correlation_spectra(1)
            convolve(0)
            rank(1)
            convolve(1)
            weight_combinations(1)
            residual(0)
            token_variances(0)
            roots(0, "rs2_ok", "newton2_ok")
            weights_low(1)
            tokens_low(0)
            residual(1)
            router(0)
            for b in range(B):
                select(b, 0, (0, 1))
                if b + 2 < B:
                    convolve(b + 2)
                select(b, 0, (2, 3))
                if b + 1 < B and b > 0:
                    residual(b + 1)
                select(b, 1, (0, 1))
                if b + 1 < B:
                    token_variances(b + 1)
                select(b, 1, (2, 3))
                if b + 1 < B:
                    roots(b + 1, "rs2_ok", "newton2_ok")
                select(b, 2, (0, 1))
                select(b, 2, (2, 3))
                if b + 1 < B:
                    tokens_low(b + 1)
                select(b, 3, (0, 1))
                if b + 1 < B:
                    router(b + 1)
                select(b, 3, (2, 3))

        @block.tensor
        def _(pe):
            matmul = nc.tensor.matmul

            def transform(ps, rows, part, done):
                matmul(ps[0:rows, 2 * P:], part(2), fwd[:, 2 * P:4 * P], start=True, stop=False)
                matmul(ps[0:rows, 2 * P:], part(3), fwd[:, 4 * P:6 * P], start=False, stop=True)
                matmul(ps[0:rows, 0:P], part(0), fwd[:, 0:P], start=True, stop=True)
                matmul(ps[0:rows, P:2 * P], part(1), fwd[:, P:2 * P], start=True, stop=True).then_inc(s[done], 1)

            def project(ps, n, m, hi, lo, hi_ok, lo_ok, b, done):
                cols = slice(m * P, (m + 1) * P)
                for c in range(C):
                    wait(pe, hi_ok, b, c + 1)
                    matmul(ps[:, :], w_hi[:, n, c, cols], hi[:, c], start=(c == 0), stop=False)
                for c in range(C):
                    matmul(ps[:, :], w_lo[:, n, c, cols], hi[:, c], start=False, stop=False)
                for c in range(C):
                    wait(pe, lo_ok, b, c + 1)
                    matmul(ps[:, :], w_hi[:, n, c, cols], lo[:, c], start=False, stop=False)
                row = slice(32 * n, 32 * n + 1)
                matmul(ps[:, 0:2], bias[row, cols], crow[row, 0:2], start=False, stop=True).then_inc(s[done], 1)

            def x_spectrum(b):
                wait(pe, "xc_ok", b)
                for c in range(C):
                    wait(pe, "xlo_ok", b - 1, c + 1) if b < 3 else wait(pe, "clo_ok", b - 1, c + 1)
                    transform(x_spec_ps[c], P, lambda k: xc[:, b % 2, k, c * P:(c + 1) * P], "xspec_done")

            def c_spectrum(b):
                wait(pe, "cc_ok", b)
                for c in range(C):
                    if b >= 2:
                        wait(pe, "xlo_ok", b, c + 1)
                    transform(c_spec_ps[b][c], P, lambda k: cc[:, b % 2, k, c * P:(c + 1) * P], "cspec_done")

            def k_spectrum(b):
                for m in range(C):
                    wait(pe, "clo_ok", 1, m + 1) if b == 0 else wait(pe, "k_ok", b - 1, m + 1)
                    if b >= 2:
                        wait(pe, "v_ok", b - 2, m + 1)
                    project(k_ps[m], 1, m, c_hi[:, b], c_lo[:, b], "chi_ok", "clo_ok", b, "k_done")

            def q_spectrum(b):
                for m in range(C):
                    wait(pe, "clo_ok", 0, m + 1) if b == 0 else wait(pe, "m_ok", b - 1, 3 * m + 3)
                    project(q_ps[m], 0, m, x_hi[:, b % 2], x_lo[:, b % 2], "xhi_ok", "xlo_ok", b, "q_done")

            def v_spectrum(b):
                for m in range(C):
                    wait(pe, "k_ok", (1, 2, 3, 3)[b], m + 1)
                    wait(pe, "v_ok", b - 1, m + 1)
                    project(v_ps[m], 2, m, c_hi[:, b], c_lo[:, b], "chi_ok", "clo_ok", b, "v_done")

            def head_sums(b):
                wait(pe, "prod_ok", b)
                if b == 2:
                    wait(pe, "cspec_ok", 0)
                for c in range(C):
                    for g in range(G):
                        col = g * ROWS + b * H + c * HC
                        mm = matmul(corr_spec_ps[:, col:col + HC], prod[:, b % 2, c, g].rearrange("p r j -> p (r j)"), hones,
                                    start=True, stop=True)
                mm.then_inc(s["sum_done"], 1)

            def correlations(r):
                pe.wait_ge(s["inv_in"], 16)
                wait(pe, "cspec_ok", r)
                wait(pe, "wflo_ok", r - 1)
                for g in range(G):
                    mm = matmul(corr_ps[0:PAIR, :], corr_spec[:, g], inv[:, g], start=(g == 0), stop=(g == G - 1))
                mm.then_inc(s["corr_done"], 1)

            def turn_weights(r):
                wait(pe, "w_ok", r)
                for q in range(S):
                    mm = nc.tensor.transpose(wt_ps[:, q * PAIR:(q + 1) * PAIR], w_sb[:, q * P:(q + 1) * P], idn[0:PAIR, 0:PAIR])
                mm.then_inc(s["wt_done"], 1)

            def weight_spectrum(r):
                wait(pe, "wc_ok", r)
                transform(wf_ps, PAIR, lambda k: wc[:, k], "wf_done")

            def spread_weights(b):
                pe.wait_ge(s["pick_ok"], 1)
                wait(pe, "wflo_ok", b // 2)
                for c in range(C):
                    wait(pe, "n_ok", b - 1, 3 * c + 3)
                    if b == 2:
                        wait(pe, ("res1_ok", "res2_ok")[c], 1)
                    matmul(wspec_ps[c][:, :], pick[:, b % 2, c], wf_hi[:, :], start=True, stop=False)
                    matmul(wspec_ps[c][:, :], pick[:, b % 2, c], wf_lo[:, :], start=False, stop=True).then_inc(s["wspec_done"], 1)

            def output_spectrum(b):
                wait(pe, "vp_ok", b)
                for h in range(2):
                    if b == 1:
                        wait(pe, "v_ok", B - 1, h + 1)
                    elif b >= 2:
                        wait(pe, "tlo_ok", b - 1, h + 1)
                    for g in (2 * h, 2 * h + 1):
                        ps = y_ps[b][h][:, g % 2 * D:g % 2 * D + D]
                        for c in range(C):
                            mm = matmul(ps, prod[:, b % 2, c, g].rearrange("p r j -> p (r j)"), w_raw[:, 3, c],
                                        start=(c == 0), stop=(g > 0 and c == C - 1))
                        if g == 0:
                            mm = matmul(ps, crow[96:97, :], bias[96:97, :], start=False, stop=True)
                    mm.then_inc(s["y_done"], 1)

            def back_to_time(b):
                for h, (ps, done) in enumerate(((even_ps[b], "even_done"), (odd_ps[b], "odd_done"))):
                    wait(pe, "y_ok", b, h + 1)
                    if b == 1:
                        wait(pe, "n_ok", 1, 3 * h + 3)
                    for n in range(2):
                        for g in (2 * h, 2 * h + 1):
                            mm = matmul(ps[:, n * D:(n + 1) * D], inv[:, g, n * P:(n + 1) * P], y_sb[:, b % 2, g],
                                        start=(g == 2 * h), stop=(g == 2 * h + 1))
                    mm.then_inc(s[done], 1)

            def turn_tokens(b):
                for c in range(C):
                    wait(pe, "xn2_ok", b)
                    for t in range(S):
                        mm = nc.tensor.transpose(turned_ps[c][:, t * P:(t + 1) * P], xn2[:, b % 2, t, c * P:(c + 1) * P], idn)
                    mm.then_inc(s["turned_done"], 1)

            def logits(b):
                wait(pe, "thi_ok", b)
                pe.wait_ge(s["rwlo_ok"], 1)
                wait(pe, "bias_ok", b - 1)
                wait(pe, "wflo_ok", 1)
                wait(pe, "tlo_ok", b)
                for t in range(S):
                    cols = slice(t * P, (t + 1) * P)
                    ps = logit_ps[:, t * 2 * E:(t + 1) * 2 * E]
                    for c in range(C):
                        matmul(ps, t_hi[:, b, c, cols], rw_sb[:, c].rearrange("p k e -> p (k e)"), start=(c == 0), stop=False)
                    for c in range(C):
                        mm = matmul(ps[:, 0:E], t_lo[:, b, c, cols], rw_sb[:, c, 0], start=False, stop=(c == C - 1))
                mm.then_inc(s["logit_done"], 1)

            def masks(b):
                wait(pe, "mask_ok", b)
                nc.tensor.transpose(mt_ps, mask[:, :, :].rearrange("p s e -> p (s e)"), idn).then_inc(s["mt_done"], 1)

            def expert_bias(b, t):
                rows = slice(32 * t, 32 * t + 32)
                wait(pe, "mt_ok", b)
                pe.wait_ge(s["eb_ok"], 1)
                wait(pe, "bias_ok", b, t)
                matmul(ebias_ps, mt[rows, :], eb_sb[rows, :], start=True, stop=True).then_inc(s["ebias_done"], 1)

            def experts(b, t, pairs):
                cols = slice(t * P, (t + 1) * P)
                for e in pairs:
                    n = (b * S + t) * PAIRS + e
                    if n >= RING:
                        pe.wait_ge(s["sel_ok"], 2 * (n - RING + 1))
                    terms = [(a[:, b, c, cols], w[:, c * PAIRS + e]) for c in range(C) for a, w in ((t_hi, ew_hi), (t_hi, ew_lo), (t_lo, ew_hi))]
                    for k, (a, w) in enumerate(terms):
                        mm = matmul(expert_ps[n % RING][:, :], a, w, start=(k == 0), stop=(k == len(terms) - 1))
                    mm.then_inc(s["expert_done"], 1)

            pe.wait_ge(s["table_in"], 16)
            x_spectrum(0)
            c_spectrum(0)
            x_spectrum(1)
            c_spectrum(1)
            pe.wait_ge(s["small_in"], 16)
            pe.wait_ge(s["wlo_ok"], 2)
            k_spectrum(0)
            q_spectrum(0)
            x_spectrum(2)
            k_spectrum(1)
            c_spectrum(2)
            q_spectrum(1)
            x_spectrum(3)
            head_sums(0)
            pe.wait_ge(s["ewlo_ok"], C * PAIRS)
            pe.wait_ge(s["wlo_ok"], 3)
            v_spectrum(0)
            c_spectrum(3)
            head_sums(1)
            k_spectrum(2)
            correlations(0)
            q_spectrum(2)
            v_spectrum(1)
            turn_weights(0)
            k_spectrum(3)
            q_spectrum(3)
            weight_spectrum(0)
            head_sums(2)
            spread_weights(0)
            v_spectrum(2)
            head_sums(3)
            correlations(1)
            output_spectrum(0)
            spread_weights(1)
            back_to_time(0)
            turn_weights(1)
            v_spectrum(3)
            weight_spectrum(1)
            output_spectrum(1)
            turn_tokens(0)
            back_to_time(1)
            logits(0)
            for b in range(B):
                experts(b, 0, (0, 1))
                masks(b)
                if b + 2 < B:
                    spread_weights(b + 2)
                if 1 <= b and b + 1 < B:
                    output_spectrum(b + 1)
                expert_bias(b, 0)
                experts(b, 0, (2, 3))
                expert_bias(b, 1)
                if 1 <= b and b + 1 < B:
                    back_to_time(b + 1)
                experts(b, 1, (0, 1))
                expert_bias(b, 2)
                experts(b, 1, (2, 3))
                expert_bias(b, 3)
                experts(b, 2, range(PAIRS))
                if b + 1 < B:
                    turn_tokens(b + 1)
                experts(b, 3, (0, 1))
                if b + 1 < B:
                    logits(b + 1)
                experts(b, 3, (2, 3))


_INS = ("x", "ctx", "wqk", "wvo", "ew", "fwd_table", "inv_table", "small_in", "counts", "head_pick")


def kernel(x, ctx_1024, g_xattn, g_ffn, L0_xattn_Wq, L0_xattn_bq, L0_xattn_Wk, L0_xattn_bk, L0_xattn_Wv, L0_xattn_bv,
           L0_xattn_Wo, L0_xattn_bo, L0_ffn_router_w, L0_ffn_router_b, L0_ffn_expert_w, L0_ffn_expert_b):
    import concourse.bacc as _bacc
    from concourse.bass_utils import run_bass_kernel_spmd as _run

    def turned(w):
        w = np.asarray(w)
        return w.T.reshape(C, P, w.shape[0]).transpose(1, 0, 2)

    fwd_table, inv_table = dft_tables()
    experts = np.asarray(L0_ffn_expert_w).transpose(2, 0, 1).reshape(C, P, E, D).transpose(1, 0, 2, 3).reshape(P, C * PAIRS, 2 * D)
    wqk, wvo = (np.stack([turned(a), turned(b)], 1) for a, b in ((L0_xattn_Wq, L0_xattn_Wk), (L0_xattn_Wv, L0_xattn_Wo)))
    rows = np.arange(P)
    everywhere = lambda a: np.broadcast_to(np.asarray(a).reshape(1, -1), (P, np.asarray(a).size))
    attention_biases = np.repeat(np.stack([np.asarray(a) for a in (L0_xattn_bq, L0_xattn_bk, L0_xattn_bv, L0_xattn_bo)]), P // 4, 0)
    small = dict(
        hones=rows[:, None] // DK == np.arange(HC)[None],
        crow=everywhere(L * (rows == 0)),
        idn=np.eye(P),
        order=everywhere(np.arange(E, 0, -1)),
        parts=np.stack([rows % 32 // E == 0, rows % 32 // E == 1], 1),
        rb=everywhere(L0_ffn_router_b),
        gates=np.concatenate([everywhere(g_xattn), everywhere(g_ffn)], 1),
        bias=attention_biases,
        rw=turned(L0_ffn_router_w).reshape(P, C * E),
        eb=np.tile(np.asarray(L0_ffn_expert_b), (P // E, 1)))
    small = np.concatenate([small[n].astype(np.float32) for n in SMALL], 1)
    counts = np.broadcast_to(np.arange(L, dtype=np.float32), (PAIR, L))
    heads = np.arange(PAIR)[:, None, None, None] == np.arange(2)[:, None, None] * H + np.arange(C)[:, None] * HC + rows // DK
    head_pick = heads.reshape(PAIR, 2 * C * P).astype(np.float32)
    arrays = dict(zip(_INS, (x, ctx_1024, wqk, wvo, experts, fwd_table, inv_table, small, counts, head_pick)))
    arrays = {n: np.ascontiguousarray(a) for n, a in arrays.items()}
    nc = _bacc.Bacc("TRN2", target_bir_lowering=False, num_devices=1)
    aps = {n: nc.dram_tensor(n + "_dram", a.shape, mybir.dt.from_np(a.dtype), kind="ExternalInput").ap() for n, a in arrays.items()}
    out = nc.dram_tensor("out_dram", (B, L, D), F32, kind="ExternalOutput").ap()
    build(nc, **aps, out=out)
    r = _run(nc, [{n + "_dram": a for n, a in arrays.items()}], core_ids=[0])
    return r.results[0]["out_dram"]
```

```python
from contextlib import ExitStack

import numpy as np

import concourse.bass as bass
from concourse import mybir

P = 128
B, L, D = 4, 512, 256
H, DK = 16, 16
E = 8
S = L // P
C = D // P
G = 4
J = 64
HC = P // DK
ROWS = B * H
PAIR = 2 * H
TILES = 2 * S
BLOCKS = TILES + E - 1
PAIRS = (BLOCKS + 1) // 2
RING = 3
TOPK = 6
EPS = 1e-5
F32 = mybir.dt.float32
F32R = mybir.dt.float32r
U32 = mybir.dt.uint32
BF16 = mybir.dt.bfloat16
ALU = mybir.AluOpType
ACT = mybir.ActivationFunctionType
AX_X = mybir.AxisListType.X
SMALL = dict(hones=HC, crow=P, idn=P, order=E, parts=2, rb=E, gates=2, bias=D, rw=C * E, eb=D)
TABLES = dict(before=P, ones=P, step=E, lower=E * E, number=BLOCKS)
PER_ROUND = dict(
    stats_ok=S, aggr_ok=S, var_ok=1, ln_ok=1, rs_ok=1, newton_ok=4, xn_ok=S, half_ok=1, xc_ok=3,
    chalf_ok=1, cc_ok=3, xspec_done=C, cspec_done=C, xhi_ok=C, xlo_ok=C, chi_ok=C, clo_ok=C,
    q_done=C, k_done=C, k_ok=C, m_ok=3 * C, prod0_ok=2, prod_ok=1, sum_done=1, v_done=C, v_ok=C,
    wspec_done=C, n_ok=3 * C, vp0_ok=2, vp_ok=1, y_done=2, y_ok=2, even_done=1, odd_done=1, res1_ok=2, res2_ok=2,
    stats2_ok=S, aggr2_ok=S, var2_ok=1, ln2_ok=1, rs2_ok=1, newton2_ok=4, xn2_ok=S,
    turned_done=C, t_ok=C, logit_done=1, ebias_done=S, bias_ok=S,

    lg_ok=1, lmax_ok=1, shift_ok=1, prob_ok=1, psum_ok=1, rden_ok=1, first_ok=1, big_ok=1, cw_ok=1, mask_ok=3,
    rank_done=1, slot_ok=10, index_ok=1, owner_ok=1, expert_ok=1, block_turned=PAIRS, bhi_ok=PAIRS, blo_ok=PAIRS,
    block_done=PAIRS, y_out_ok=PAIRS, stored0=32, stored1=32, stored2=32, stored3=32, xs_in0=32, xs_in1=32,
    mt_done=1, mt_ok=1, sum_ok=TILES,
    cspec_ok=1, corr_done=1, corr_ok=1, top_ok=1, topi_ok=1, lasti_ok=1, wmax_ok=1, exp_ok=1, keep1_ok=1, keep2_ok=1,
    keep3_ok=1, wsum_ok=1, wr_ok=1, w_ok=1, wt_done=1, wt_ok=1, whalf_ok=1, wc_ok=3, wf_done=1, wfhi_ok=1, wflo_ok=1)
ONCE = """table_in small_in wqk_in wvo_in inv_in cnt_in pick_in ew_in gate_ok cleared tables_in scattered0 scattered1 out_done tables_ok whi_ok wlo_ok pick_ok
    ewhi_ok ewlo_ok ebhi_ok eblo_ok ebpart_ok eb_ok zero_ok""".split()


def after(name, r, k=None):
    n = PER_ROUND[name]
    return r * n + (n if k is None else k)


def dft_tables():
    t = np.arange(L)
    j = np.arange(J)
    f = [4 * j, 4 * j + 2, 4 * j + 1, 4 * j + 3]

    def angle(times, freqs):
        return 2 * np.pi * ((times[:, None] * freqs[None, :]) % L) / L

    q = t[:P]
    forward = []
    for g in (0, 1):
        a = angle(q, f[g])
        re, im = np.cos(a), -np.sin(a)
        if g == 0:
            im[:, 0] = np.where(q % 2 == 0, 1.0, -1.0)
        forward += [re, im]
    for g in (2, 3):
        a = angle(q, f[g])
        forward += [np.cos(a), -np.sin(a)]
    for g, sign in ((2, -1.0), (3, 1.0)):
        a = angle(q, f[g])
        forward += [sign * np.sin(a), sign * np.cos(a)]
    inverse = np.zeros((2, J, G, L))
    for g in range(G):
        a = angle(t, f[g]).T
        inverse[0, :, g] = 2.0 * np.cos(a) / L
        inverse[1, :, g] = -2.0 * np.sin(a) / L
    inverse[0, 0, 0] = 1.0 / L
    inverse[1, 0, 0] = np.where(t % 2 == 0, 1.0, -1.0) / L
    return (np.concatenate(forward, 1).astype(np.float32),
            inverse.reshape(P, G * L).astype(np.float32))


def build(nc, x, ctx, wqk, wvo, ew, fwd_table, inv_table, small_in, counts, head_pick, sort_tables, out):
    es = ExitStack()
    with es:
        def sb(name, shape, dt=F32):
            return es.enter_context(nc.sbuf_tensor(name, shape, dt))

        bank = [es.enter_context(nc.psum_tensor(f"bank{n}", [P, 512], F32)) for n in range(8)]
        x_spec_ps = bank[0:2]
        c_spec_ps = [bank[2:4], bank[6:8], bank[0:2], bank[0:2]]
        q_ps = bank[2:4]
        k_ps = v_ps = bank[4:6]
        corr_spec_ps = bank[6]
        corr_ps = bank[7]
        wt_ps = bank[7]
        wf_ps = bank[7]
        wspec_ps = bank[0:2]
        y_ps = [bank[2:4], bank[4:6]] * 2
        even_ps = [bank[2], bank[4]] * 2
        odd_ps = [bank[3], bank[5]] * 2
        turned_ps = bank[6]
        logit_ps = bank[7][:, 0:TILES * E]
        rank_ps = bank[7][:, P:P + (TILES + 1) * E]
        mt_ps = bank[0][:, 0:2 * P]
        ebias_ps = bank[0:2]
        block_ps = [bank[n] for n in (2, 3, 6)]
        expert_ps = [bank[n] for n in (4, 5, 7)]

        fwd = sb("fwd", [P, 6 * P])
        inv = sb("inv", [P, G, L])
        small = sb("small", [P, sum(SMALL.values())])
        part = {}
        for name, width in SMALL.items():
            start = sum(w for n, w in SMALL.items() if n in part)
            part[name] = small[:, start:start + width]
        hones = part["hones"]
        crow = part["crow"]
        idn = part["idn"]
        order = part["order"]
        parts = part["parts"]
        bias = part["bias"]
        gates = part["gates"]
        rb_sb = part["rb"]
        rw_raw = part["rw"].rearrange("p (c e) -> p c e", c=C)
        eb_raw = part["eb"]
        pick = sb("pick", [PAIR, 2, C, P], F32R)
        w_raw = sb("w_raw", [P, 4, C, D])
        w_hi = sb("w_hi", [P, 3, C, D], F32R)
        w_lo = sb("w_lo", [P, 3, C, D], F32R)
        ew_raw = sb("ew_raw", [P, C * E // 2, 2 * D])
        ew_hi = sb("ew_hi", [P, C * E // 2, 2 * D], F32R)
        ew_lo = sb("ew_lo", [P, C * E // 2, 2 * D], F32R)
        eb_sb = sb("eb_sb", [P, D], F32R)
        tg = sb("tg", [P, 3])

        x_sb = sb("x_sb", [P, B, S, D])
        ctx_sb = sb("ctx_sb", [P, 2, S, D])
        stats = sb("stats", [P, S, 6])
        mv = sb("mv", [P, 2, S, 2])
        root = sb("root", [P, 2, 5, S])
        xn = sb("xn", [P, S, D])
        half = sb("half", [P, 2, D])
        chalf = sb("chalf", [P, 2, D])
        xc = sb("xc", [P, 2, 4, D])
        cc = sb("cc", [P, 2, 4, D])
        x_hi = sb("x_hi", [P, 2, C, L], F32R)
        x_lo = sb("x_lo", [P, 2, C, L], F32R)
        c_hi = sb("c_hi", [P, B, C, L], F32R)
        c_lo = sb("c_lo", [P, B, C, L], F32R)
        k_sb = sb("k_sb", [P, C, L])
        m1 = sb("m1", [P, C, G, 2, J])
        m2 = sb("m2", [P, C, G, 2, J])
        prod = sb("prod", [P, 2, C, G, 2, J])
        v_sb = ew_raw[:, :, :].rearrange("p (b c) l -> p b c l", b=B)
        corr_spec = xn[:, 0, 0:G * PAIR].rearrange("p (g r) -> p g r", g=G)
        corr = xn[0:PAIR, 0:2].rearrange("p a d -> p (a d)")
        ex = xn[0:PAIR, 2:4].rearrange("p a d -> p (a d)")
        keep = half[0:PAIR, :, :].rearrange("p a d -> p (a d)")
        w_sb = chalf[0:PAIR, :, :].rearrange("p a d -> p (a d)")
        top = sb("top", [PAIR, 8])
        topi = sb("topi", [PAIR, 8], U32)
        last = sb("last", [PAIR, 4])
        wt = w_raw[:, 2, 1, 0:S * PAIR].rearrange("p (s r) -> p s r", s=S)
        whalf = half[:, 0, 0:2 * PAIR].rearrange("p (s r) -> p s r", s=2)
        wc = chalf[:, 0, 0:4 * PAIR].rearrange("p (k r) -> p k r", k=4)
        wf_hi = sb("wf_hi", [PAIR, L], F32R)
        wf_lo = sb("wf_lo", [PAIR, L], F32R)
        cnt = w_raw[0:PAIR, 1].rearrange("p c d -> p (c d)")
        pick_raw = w_raw[0:PAIR, 0].rearrange("p c d -> p (c d)")
        eb_lo = w_raw[:, 2, 0]

        y_sb = ctx_sb
        xn2 = [xc[:, 0], xc[:, 1], cc[:, 0], cc[:, 1]]
        t_sb = [k_sb[:, :, :], xn[:, :, :].rearrange("p s d -> p (s d)").rearrange("p (c l) -> p c l", c=C)]
        tables = half[:, :, :].rearrange("p a d -> p (a d)")
        table = {}
        for name, width in TABLES.items():
            start = sum(w for n, w in TABLES.items() if n in table)
            table[name] = tables[:, start:start + width]
        counters = tables[:, 3 * P - 32:4 * P - 32].bitcast(BF16).rearrange("p (k m) -> p k m", k=2)
        chosen = tables[:, 4 * P - 32:].bitcast(BF16)
        mask = fwd[:, 0:B * S * 32].rearrange("p (b s e) -> p b s e", b=B, s=S)
        zero = sb("zero", [P, P])
        lg = chalf[:, 1].rearrange("p (k t e) -> p k t e", k=4, t=TILES)
        col = sb("col", [P, 4, TILES])
        cw = sb("cw", [P, B, S])
        mt = sb("mt", [P, 2, P], F32R)
        rank_sb = fwd[:, 4 * P:4 * P + (TILES + 1) * E]
        grid = fwd[:, 5 * P:5 * P + BLOCKS * E]
        nblocks = sb("nblocks", [P, 3, E])
        slot = sb("slot", [P, TILES])
        index = sb("index", [P, 2, TILES], U32)
        whose = sb("whose", [P, BLOCKS])
        whose_int = sb("whose_int", [P, 2, 16], U32)
        xs = ctx_sb[:, :, :, :].rearrange("p a s d -> p (a s) d")
        b_hi = c_hi[:, 0:2].rearrange("p b c l -> p (b c) l")
        b_lo = c_lo[:, 0:2].rearrange("p b c l -> p (b c) l")
        ys = prod[:, :, :, :, :, :].rearrange("p b c g r j -> p (b c g r j)").rearrange("p (k l) -> p k l", k=4)
        quads = [m1[:, :, :, :, :].rearrange("p c g r j -> p (c g r j)").rearrange("p (t d) -> p t d", d=D),
                 m2[:, :, :, :, :].rearrange("p c g r j -> p (c g r j)").rearrange("p (t d) -> p t d", d=D),
                 w_raw[:, 0:2].rearrange("p a c d -> p (a c) d"),
                 k_sb[:, :, :].rearrange("p c l -> p (c l)").rearrange("p (t d) -> p t d", d=D)]
        yg = [[quads[2 * r + t // 4][:, t % 4] for t in range(TILES)] for r in range(2)]
        gathered = [[es.enter_context(nc.semaphore(f"gathered{r}_{t}")) for t in range(TILES)] for r in range(2)]
        sorted_x = [nc.dram_tensor(f"sorted_x{r}", (BLOCKS * P, D), F32, kind="Internal").ap() for r in range(2)]
        sorted_y = [nc.dram_tensor(f"sorted_y{r}", (BLOCKS * P, D), F32, kind="Internal").ap() for r in range(2)]

        s = {n: es.enter_context(nc.semaphore(n)) for n in (*PER_ROUND, *ONCE)}
        x_in = [es.enter_context(nc.semaphore(f"x_in{b}")) for b in range(B)]
        c_in = [es.enter_context(nc.semaphore(f"c_in{b}")) for b in range(B)]
        block = es.enter_context(nc.Block())

        def wait(eng, name, r, k=None):
            if after(name, r, k) > 0:
                eng.wait_ge(s[name], after(name, r, k))

        def f32(t):
            return t.bitcast(F32)

        @block.sync
        def _(sp):
            def load_x(b):
                sp.dma_start(x_sb[:, b], x[b].rearrange("(s p) d -> p s d", p=P)).then_inc(x_in[b], 16)

            def load_context(b):
                wait(sp, "cc_ok", b - 2)
                sp.dma_start(ctx_sb[:, b % 2], ctx[b].rearrange("(s p) d -> p s d", p=P)).then_inc(c_in[b], 16)

            load_x(0)
            load_context(0)
            sp.dma_start(fwd[:, :], fwd_table).then_inc(s["table_in"], 16)
            load_x(1)
            sp.dma_start(w_raw[:, 0:2], wqk).then_inc(s["wqk_in"], 16)
            sp.dma_start(small[:, :], small_in).then_inc(s["small_in"], 16)
            load_context(1)
            sp.dma_start(w_raw[:, 2:4], wvo).then_inc(s["wvo_in"], 16)
            load_x(2)
            sp.dma_start(ew_raw[:, :, :], ew).then_inc(s["ew_in"], 16)
            load_context(2)
            load_x(3)
            sp.dma_start(inv[:, :, :], inv_table.rearrange("p (g t) -> p g t", g=G)).then_inc(s["inv_in"], 16)
            load_context(3)
            sp.wait_ge(s["wlo_ok"], 1)
            sp.dma_start(pick_raw, head_pick).then_inc(s["pick_in"], 16)
            sp.wait_ge(s["wlo_ok"], 2)
            sp.dma_start(cnt, counts).then_inc(s["cnt_in"], 16)
            sp.wait_ge(s["zero_ok"], 1)
            for r in range(2):
                sp.dma_start(sorted_x[r].rearrange("(p n) d -> p (n d)", p=P).rearrange("p (k d) -> p k d", d=P),
                             zero[:, :].unsqueeze(1).to_broadcast([P, BLOCKS * D // P, P])).then_inc(s["cleared"], 16)
            wait(sp, "wc_ok", 1)
            sp.dma_start(tables[:, 0:sum(TABLES.values())], sort_tables).then_inc(s["tables_in"], 16)
            wait(sp, "odd_done", B - 1)
            for r in range(2):
                for k in range(4):
                    sp.wait_ge(s[f"scattered{r}"], 16 * TILES)
                    wait(sp, "block_turned", r, 2 * (k - 1)) if k >= 2 else wait(sp, "block_turned", r - 1)
                    n = min(4, BLOCKS - 4 * k)
                    sp.dma_start(xs[:, 4 * (k % 2):4 * (k % 2) + n],
                                 sorted_x[r][4 * k * P:(4 * k + n) * P].rearrange("(n p) d -> p n d", p=P)).then_inc(s[f"xs_in{k % 2}"], 16)
            for b in range(B):
                for t in range(S):
                    wait(sp, "sum_ok", b // 2, b % 2 * S + t + 1)
                    sp.dma_start(out[b, t * P:(t + 1) * P, :], x_sb[:, b, t]).then_inc(s["out_done"], 16)
            sp.wait_ge(s["out_done"], 16 * B * S)

        @block.gpsimd
        def _(pool):
            def context(b):
                p = b % 2
                pool.wait_ge(c_in[b], 16)
                wait(pool, "cspec_done", b - 2)
                pool.tensor_tensor(cc[:, p, 2:4], ctx_sb[:, p, 0:2], ctx_sb[:, p, 2:4], ALU.subtract).then_inc(s["cc_ok"], 1)
                pool.tensor_tensor(chalf[:, :, :], ctx_sb[:, p, 0:2], ctx_sb[:, p, 2:4], ALU.add).then_inc(s["chalf_ok"], 1)
                wait(pool, "chalf_ok", b)
                pool.tensor_tensor(cc[:, p, 0], chalf[:, 0], chalf[:, 1], ALU.add).then_inc(s["cc_ok"], 1)
                pool.tensor_tensor(cc[:, p, 1], chalf[:, 0], chalf[:, 1], ALU.subtract).then_inc(s["cc_ok"], 1)
                wait(pool, "cc_ok", b)

            def weights_low(n):
                pool.wait_ge(s["whi_ok"], n + 1)
                pool.tensor_tensor(w_lo[:, n], w_raw[:, n], f32(w_hi[:, n]), ALU.subtract).then_inc(s["wlo_ok"], 1)

            def spectra(m):
                return m.rearrange("p c g r j -> p (c g) r j")

            def real(b, a, done, op):
                a, o = spectra(a[:, :, :, :, :]), spectra(prod[:, b % 2])
                pool.tensor_tensor(o[:, :, 0], a[:, :, 0], a[:, :, 1], op).then_inc(s[done], 1)

            def ends(b, done):
                pool.tensor_copy(prod[:, b % 2, :, 0, :, 0], m1[:, :, 0, :, 0]).then_inc(s[done], 1)

            def correlate(b):
                wait(pool, "sum_done", b - 2)
                wait(pool, "m_ok", b)
                real(b, m1, "prod0_ok", ALU.add)
                m, o = spectra(m2[:, :, :, :, :]), spectra(prod[:, b % 2])
                pool.tensor_tensor(o[:, :, 1], m[:, :, 1], m[:, :, 0], ALU.subtract).then_inc(s["prod0_ok"], 1)
                wait(pool, "prod0_ok", b)
                ends(b, "prod_ok")

            def convolve(b):
                wait(pool, "sum_done", B - 1) if b < 2 else wait(pool, "y_done", b - 2)
                wait(pool, "n_ok", b)
                real(b, m1, "vp0_ok", ALU.subtract)
                wait(pool, "vp0_ok", b)
                ends(b, "vp_ok")

            def scatter(r):
                pool.wait_ge(s["cleared"], 32)
                wait(pool, "index_ok", r)
                for t in range(TILES):
                    wait(pool, "xn2_ok", 2 * r + t // S)
                    pool.indirect_dma_start(sorted_x[r], bass.IndirectOffsetOnAxis(index[:, r, t:t + 1], 0),
                                            xn2[2 * r + t // S][:, t % S], None).then_inc(s[f"scattered{r}"], 16)

            def gather(r):
                for k in range(4):
                    wait(pool, f"stored{k}", r)
                for t in range(TILES):
                    pool.indirect_dma_start(yg[r][t], None, sorted_y[r],
                                            bass.IndirectOffsetOnAxis(index[:, r, t:t + 1], 0)).then_inc(gathered[r][t], 16)

            pool.memset(zero[:, :], 0.0).then_inc(s["zero_ok"], 1)
            context(0)
            weights_low(0)
            weights_low(1)
            context(1)
            weights_low(2)
            context(2)
            context(3)
            for b in range(B):
                correlate(b)
            for b in range(B):
                if b == 2:
                    wait(pool, "wf_done", 1)
                    pool.memset(mask, 0.0).then_inc(s["zero_ok"], 1)
                convolve(b)
            scatter(0)
            scatter(1)
            gather(0)
            gather(1)

        @block.scalar
        def _(act):
            act.preload_act_table_set("natural_log_exp_and_others")

            def log_root(b, var_ok, ln_ok, rs_ok):
                wait(act, var_ok, b)
                act.activation(root[:, b % 2, 1], root[:, b % 2, 0], ACT.Ln).then_inc(s[ln_ok], 1)
                wait(act, ln_ok, b)
                act.activation(root[:, b % 2, 2], root[:, b % 2, 1], ACT.Exp, scale=-0.5).then_inc(s[rs_ok], 1)

            def normalise(p, dst, src, done, tiles=range(S)):
                for t in tiles:
                    act.activation(dst(t), src(t), ACT.Identity, bias=root[:, p, 4, t:t + 1], scale=root[:, p, 3, t:t + 1]).then_inc(s[done], 1)

            def normalise_x(b):
                wait(act, "newton_ok", b)
                wait(act, "xc_ok", b - 1)
                normalise(b % 2, lambda t: xn[:, t], lambda t: x_sb[:, b, t], "xn_ok", range(2 if b < 2 else S))

            def normalise_tokens(b):
                wait(act, "newton2_ok", b)
                normalise(b % 2, lambda t: xn2[b][:, t], lambda t: x_sb[:, b, t], "xn2_ok")

            def split_weight(n):
                act.copy(w_hi[:, n], w_raw[:, n]).then_inc(s["whi_ok"], 1)

            def split_experts(ks):
                for k in ks:
                    act.copy(ew_hi[:, k], ew_raw[:, k]).then_inc(s["ewhi_ok"], 1)

            def x_spectrum(b):
                wait(act, "q_done", b - 2)
                for c in range(C):
                    wait(act, "xspec_done", b, c + 1)
                    act.copy(x_hi[:, b % 2, c], x_spec_ps[c][:, :]).then_inc(s["xhi_ok"], 1)

            def c_spectrum(b):
                for c in range(C):
                    wait(act, "cspec_done", b, c + 1)
                    act.copy(c_hi[:, b, c], c_spec_ps[b][c][:, :]).then_inc(s["chi_ok"], 1)

            def k_out(b):
                wait(act, "m_ok", b - 1)
                for c in range(C):
                    wait(act, "k_done", b, c + 1)
                    act.copy(k_sb[:, c], k_ps[c][:, :]).then_inc(s["k_ok"], 1)

            def v_out(b):
                for c in range(C):
                    wait(act, "v_done", b, c + 1)
                    act.copy(v_sb[:, b, c], v_ps[c][:, :]).then_inc(s["v_ok"], 1)

            def exponentials(r):
                wait(act, "top_ok", r)
                act.mul(last[:, 1:2], top[:, 0:1], -1.0 / DK).then_inc(s["wmax_ok"], 1)
                wait(act, "wmax_ok", r)
                act.activation(ex, corr, ACT.Exp, bias=last[:, 1:2], scale=1.0 / DK).then_inc(s["exp_ok"], 1)

            def weights_out(r):
                wait(act, "wf_done", r)
                wait(act, "wspec_done", 2 * r - 1)
                act.copy(wf_hi[:, :], wf_ps[0:PAIR, :]).then_inc(s["wfhi_ok"], 1)

            def y_out(b):
                wait(act, "odd_done", b - 2)
                wait(act, "cc_ok", B - 1)
                for h in range(2):
                    wait(act, "y_done", b, h + 1)
                    act.copy(y_sb[:, b % 2, 2 * h:2 * h + 2], y_ps[b][h][:, :].rearrange("p (g d) -> p g d", g=2)).then_inc(s["y_ok"], 1)

            def tokens_out(b):
                wait(act, "m_ok", B - 1)
                wait(act, "w_ok", 1)
                wait(act, "logit_done", b - 2)
                for c in range(C):
                    wait(act, "turned_done", b, c + 1)
                    act.copy(t_sb[b % 2][:, c], turned_ps[:, :]).then_inc(s["t_ok"], 1)

            def tables_out():
                act.wait_ge(s["tables_in"], 16)
                act.copy(counters, tables[:, 0:2 * P].rearrange("p (k m) -> p k m", k=2)).then_inc(s["tables_ok"], 1)

            def router(b):
                wait(act, "shift_ok", b)
                act.activation(lg[:, 2], lg[:, 1], ACT.Exp).then_inc(s["prob_ok"], 1)

            def masks_out(r):
                wait(act, "mt_done", r)
                wait(act, "ebias_done", 2 * r - 1)
                act.copy(mt[:, :, :], mt_ps.rearrange("p (b t) -> p b t", b=2)).then_inc(s["mt_ok"], 1)

            def blocks_out(r, k):
                wait(act, "block_turned", r, k + 1)
                wait(act, "block_done", r, k - 3) if k >= 4 else wait(act, "block_done", r - 1, PAIRS - 3 + k)
                n = min(2, BLOCKS - 2 * k) * D
                act.copy(b_hi[:, k % 4, 0:n], block_ps[k % RING][:, 0:n]).then_inc(s["bhi_ok"], 1)

            def products_out(r, k):
                wait(act, "block_done", r, k + 1)
                wait(act, f"stored{k % 4}", r, 16) if k >= 4 else wait(act, f"stored{k}", r - 1)
                n = min(2, BLOCKS - 2 * k)
                act.copy(ys[:, k % 4, 0:n * D], expert_ps[k % RING][:, 0:n * D]).then_inc(s["y_out_ok"], 1)
                wait(act, "y_out_ok", r, k + 1)
                act.dma_start(sorted_y[r][2 * k * P:(2 * k + n) * P].rearrange("(n p) d -> p n d", p=P),
                              ys[:, k % 4, 0:n * D].rearrange("p (n d) -> p n d", n=n)).then_inc(s[f"stored{k % 4}"], 16)

            log_root(0, "var_ok", "ln_ok", "rs_ok")
            normalise_x(0)
            log_root(1, "var_ok", "ln_ok", "rs_ok")
            normalise_x(1)
            act.wait_ge(s["wqk_in"], 16)
            split_weight(0)
            split_weight(1)
            log_root(2, "var_ok", "ln_ok", "rs_ok")
            x_spectrum(0)
            c_spectrum(0)
            normalise_x(2)
            x_spectrum(1)
            c_spectrum(1)
            act.wait_ge(s["wvo_in"], 16)
            split_weight(2)
            act.wait_ge(s["ew_in"], 16)
            split_experts(range(0, 2))
            k_out(0)
            log_root(3, "var_ok", "ln_ok", "rs_ok")
            x_spectrum(2)
            normalise_x(3)
            c_spectrum(2)
            split_experts(range(2, 4))
            k_out(1)
            split_experts(range(4, C * E // 2))
            x_spectrum(3)
            c_spectrum(3)
            act.wait_ge(s["pick_in"], 16)
            act.copy(pick[:, :, :, :], pick_raw.rearrange("p (b c d) -> p b c d", b=2, c=C)).then_inc(s["pick_ok"], 1)
            act.wait_ge(s["small_in"], 16)
            act.copy(eb_sb[:, :], eb_raw).then_inc(s["ebhi_ok"], 1)
            v_out(0)
            exponentials(0)
            k_out(2)
            v_out(1)
            k_out(3)
            weights_out(0)
            act.activation(tg[:, 0:2], gates, ACT.Tanh).then_inc(s["gate_ok"], 1)
            act.wait_ge(s["gate_ok"], 1)
            act.mul(tg[:, 2:3], tg[:, 0:1], -1.0).then_inc(s["gate_ok"], 1)
            act.preload_act_table_set("natural_log_exp_and_others")
            v_out(2)
            exponentials(1)
            v_out(3)
            y_out(0)
            weights_out(1)
            log_root(0, "var2_ok", "ln2_ok", "rs2_ok")
            y_out(1)
            normalise_tokens(0)
            tokens_out(0)
            log_root(1, "var2_ok", "ln2_ok", "rs2_ok")
            y_out(2)
            normalise_tokens(1)
            y_out(3)
            tokens_out(1)
            log_root(2, "var2_ok", "ln2_ok", "rs2_ok")
            tables_out()
            normalise_tokens(2)
            router(0)
            tokens_out(2)
            masks_out(0)
            log_root(3, "var2_ok", "ln2_ok", "rs2_ok")
            normalise_tokens(3)
            tokens_out(3)
            router(1)
            masks_out(1)
            for r in range(2):
                blocks_out(r, 0)
                blocks_out(r, 1)
                for k in range(PAIRS):
                    if k + 2 < PAIRS:
                        blocks_out(r, k + 2)
                    products_out(r, k)

        @block.vector
        def _(dve):
            def variances(src, b, stats_ok, aggr_ok, var_ok):
                for t in range(S):
                    dve.bn_stats(stats[:, t], src(t)).then_inc(s[stats_ok], 1)
                wait(dve, stats_ok, b)
                for t in range(S):
                    dve.bn_aggr(mv[:, b % 2, t], stats[:, t]).then_inc(s[aggr_ok], 1)
                wait(dve, aggr_ok, b)
                dve.tensor_scalar(root[:, b % 2, 0], mv[:, b % 2, :, 1], EPS, None, ALU.add).then_inc(s[var_ok], 1)

            def roots(b, rs_ok, newton_ok):
                wait(dve, rs_ok, b)
                steps = root[:, b % 2]
                dve.scalar_tensor_tensor(steps[:, 1], steps[:, 2], -0.5, steps[:, 2], ALU.mult, ALU.mult).then_inc(s[newton_ok], 1)
                wait(dve, newton_ok, b, 1)
                dve.tensor_tensor(steps[:, 1], steps[:, 1], steps[:, 0], ALU.mult).then_inc(s[newton_ok], 1)
                wait(dve, newton_ok, b, 2)
                dve.scalar_tensor_tensor(steps[:, 3], steps[:, 1], 1.5, steps[:, 2], ALU.add, ALU.mult).then_inc(s[newton_ok], 1)
                wait(dve, newton_ok, b, 3)
                dve.scalar_tensor_tensor(steps[:, 4], mv[:, b % 2, :, 0], -1.0, steps[:, 3], ALU.mult, ALU.mult).then_inc(s[newton_ok], 1)

            def x_statistics(b):
                dve.wait_ge(x_in[b], 16)
                wait(dve, "xn_ok", b - 2)
                variances(lambda t: x_sb[:, b, t], b, "stats_ok", "aggr_ok", "var_ok")

            def x_roots(b):
                roots(b, "rs_ok", "newton_ok")
                if b < 2:
                    wait(dve, "newton_ok", b)
                    for t in range(2, S):
                        dve.tensor_scalar(xn[:, t], x_sb[:, b, t], mv[:, b, t, 0:1], root[:, b, 3, t:t + 1],
                                          ALU.subtract, ALU.mult).then_inc(s["xn_ok"], 1)

            def x_combinations(b):
                p = b % 2
                wait(dve, "xspec_done", b - 2)
                wait(dve, "xn_ok", b)
                dve.tensor_tensor(half[:, :, :], xn[:, 0:2], xn[:, 2:4], ALU.add).then_inc(s["half_ok"], 1)
                dve.tensor_tensor(xc[:, p, 2:4], xn[:, 0:2], xn[:, 2:4], ALU.subtract).then_inc(s["xc_ok"], 1)
                wait(dve, "half_ok", b)
                dve.tensor_tensor(xc[:, p, 0], half[:, 0], half[:, 1], ALU.add).then_inc(s["xc_ok"], 1)
                dve.tensor_tensor(xc[:, p, 1], half[:, 0], half[:, 1], ALU.subtract).then_inc(s["xc_ok"], 1)
                wait(dve, "xc_ok", b)

            def x_low(b):
                for c in range(C):
                    wait(dve, "xhi_ok", b, c + 1)
                    dve.tensor_tensor(x_lo[:, b % 2, c], x_spec_ps[c][:, :], f32(x_hi[:, b % 2, c]), ALU.subtract).then_inc(s["xlo_ok"], 1)

            def c_low(b):
                for c in range(C):
                    wait(dve, "chi_ok", b, c + 1)
                    dve.tensor_tensor(c_lo[:, b, c], c_spec_ps[b][c][:, :], f32(c_hi[:, b, c]), ALU.subtract).then_inc(s["clo_ok"], 1)

            def products(c, a_ps, k, done):
                a = a_ps[:, :].rearrange("p (g r j) -> p g r j", g=G, r=2)
                k = k.rearrange("p (g r j) -> p g r j", g=G, r=2)
                dve.tensor_tensor(m1[:, c], a, k, ALU.mult).then_inc(s[done], 1)
                dve.tensor_tensor(m2[:, c, :, 0], a[:, :, 0], k[:, :, 1], ALU.mult).then_inc(s[done], 1)
                dve.tensor_tensor(m2[:, c, :, 1], a[:, :, 1], k[:, :, 0], ALU.mult).then_inc(s[done], 1)

            def correlate(b):
                wait(dve, "prod_ok", b - 1)
                for c in range(C):
                    wait(dve, "k_ok", b, c + 1)
                    wait(dve, "q_done", b, c + 1)
                    products(c, q_ps[c], k_sb[:, c], "m_ok")

            def convolve(b, chunks=range(C)):
                for c in chunks:
                    if c == 0:
                        wait(dve, "prod_ok", B - 1)
                        wait(dve, "vp_ok", b - 1)
                    wait(dve, "wspec_done", b, c + 1)
                    wait(dve, "v_ok", b, c + 1)
                    products(c, wspec_ps[c], v_sb[:, b, c], "n_ok")
                if C - 1 in chunks:
                    wait(dve, "n_ok", b)
                    wait(dve, "sum_done", b + 2) if b < 2 else wait(dve, "y_done", b - 2)
                    m = m2[:, :, :, :, :].rearrange("p c g r j -> p (c g) r j")
                    o = prod[:, b % 2].rearrange("p c g r j -> p (c g) r j")
                    dve.tensor_tensor(o[:, :, 1], m[:, :, 1], m[:, :, 0], ALU.add).then_inc(s["vp0_ok"], 1)

            def split_experts(ks):
                for k in ks:
                    dve.wait_ge(s["ewhi_ok"], k + 1)
                    dve.tensor_tensor(ew_lo[:, k], ew_raw[:, k], f32(ew_hi[:, k]), ALU.subtract).then_inc(s["ewlo_ok"], 1)

            def correlation_spectra(r):
                wait(dve, "sum_done", 2 * r + 1)
                wait(dve, "w_ok", r - 1)
                dve.tensor_copy(corr_spec, corr_spec_ps[:, 0:G * ROWS].rearrange("p (g r) -> p g r", g=G)
                                [:, :, r * PAIR:(r + 1) * PAIR]).then_inc(s["cspec_ok"], 1)

            def rank(r):
                wait(dve, "corr_done", r)
                dve.tensor_copy(corr, corr_ps[0:PAIR, :]).then_inc(s["corr_ok"], 1)
                wait(dve, "corr_ok", r)
                dve.max(top[:, :], corr).then_inc(s["top_ok"], 1)
                wait(dve, "top_ok", r)
                dve.max_index(topi[:, :], top[:, :], corr).then_inc(s["topi_ok"], 1)
                wait(dve, "topi_ok", r)
                dve.tensor_copy(last[:, 0:1], topi[:, TOPK - 1:TOPK]).then_inc(s["lasti_ok"], 1)
                wait(dve, "lasti_ok", r)
                dve.wait_ge(s["cnt_in"], 16)
                dve.tensor_scalar(keep, cnt, last[:, 0:1], None, ALU.is_le).then_inc(s["keep1_ok"], 1)
                wait(dve, "keep1_ok", r)
                wait(dve, "wf_done", r - 1)
                dve.scalar_tensor_tensor(w_sb, corr, top[:, TOPK - 1:TOPK], keep, ALU.is_equal, ALU.mult).then_inc(s["keep2_ok"], 1)
                wait(dve, "keep2_ok", r)
                dve.scalar_tensor_tensor(keep, corr, top[:, TOPK - 1:TOPK], w_sb, ALU.is_gt, ALU.add).then_inc(s["keep3_ok"], 1)
                wait(dve, "keep3_ok", r)
                wait(dve, "exp_ok", r)
                dve.tensor_tensor_reduce(out=ex, in0=ex, in1=keep, scale=1.0, scalar=0.0,
                                         op0=ALU.mult, op1=ALU.add, accum_out=last[:, 2:3]).then_inc(s["wsum_ok"], 1)
                wait(dve, "wsum_ok", r)
                dve.reciprocal(last[:, 3:4], last[:, 2:3]).then_inc(s["wr_ok"], 1)
                wait(dve, "wr_ok", r)
                dve.tensor_scalar(w_sb, ex, last[:, 3:4], None, ALU.mult).then_inc(s["w_ok"], 1)

            def weight_combinations(r):
                wait(dve, "wt_done", r)
                dve.tensor_copy(wt, wt_ps[:, 0:S * PAIR].rearrange("p (s r) -> p s r", s=S)).then_inc(s["wt_ok"], 1)
                wait(dve, "wt_ok", r)
                dve.tensor_tensor(whalf, wt[:, 0:2], wt[:, 2:4], ALU.add).then_inc(s["whalf_ok"], 1)
                dve.tensor_tensor(wc[:, 2:4], wt[:, 0:2], wt[:, 2:4], ALU.subtract).then_inc(s["wc_ok"], 1)
                wait(dve, "whalf_ok", r)
                dve.tensor_tensor(wc[:, 0], whalf[:, 0], whalf[:, 1], ALU.add).then_inc(s["wc_ok"], 1)
                dve.tensor_tensor(wc[:, 1], whalf[:, 0], whalf[:, 1], ALU.subtract).then_inc(s["wc_ok"], 1)
                wait(dve, "wc_ok", r)

            def weights_low(r):
                wait(dve, "wfhi_ok", r)
                wait(dve, "wspec_done", 2 * r - 1)
                dve.tensor_tensor(wf_lo[:, :], wf_ps[0:PAIR, :], f32(wf_hi[:, :]), ALU.subtract).then_inc(s["wflo_ok"], 1)

            def split_biases():
                dve.wait_ge(s["ebhi_ok"], 1)
                dve.tensor_tensor(eb_lo, eb_raw, f32(eb_sb[:, :]), ALU.subtract).then_inc(s["eblo_ok"], 1)
                dve.wait_ge(s["eblo_ok"], 1)
                dve.tensor_scalar(eb_lo, eb_lo, parts[:, 1:2], None, ALU.mult).then_inc(s["ebpart_ok"], 1)
                dve.wait_ge(s["ebpart_ok"], 1)
                dve.scalar_tensor_tensor(eb_sb[:, :], f32(eb_sb[:, :]), parts[:, 0:1], eb_lo, ALU.mult, ALU.add).then_inc(s["eb_ok"], 1)

            def residual(b):
                wait(dve, "even_done", b)
                dve.wait_ge(s["gate_ok"], 2)
                for n in range(2):
                    dve.scalar_tensor_tensor(x_sb[:, b, 2 * n:2 * n + 2], even_ps[b][:, :].rearrange("p (s d) -> p s d", s=2), tg[:, 0:1],
                                             x_sb[:, b, 2 * n:2 * n + 2], ALU.mult, ALU.add).then_inc(s["res1_ok"], 1)
                wait(dve, "res1_ok", b)
                wait(dve, "odd_done", b)
                for n, k in ((0, 0), (1, 2)):
                    dve.scalar_tensor_tensor(x_sb[:, b, 2 * n:2 * n + 2], odd_ps[b][:, :].rearrange("p (s d) -> p s d", s=2), tg[:, k:k + 1],
                                             x_sb[:, b, 2 * n:2 * n + 2], ALU.mult, ALU.add).then_inc(s["res2_ok"], 1)

            def token_variances(b):
                wait(dve, "res2_ok", b)
                wait(dve, "xn_ok", B - 1)
                wait(dve, "xn2_ok", b - 2)
                variances(lambda t: x_sb[:, b, t], b, "stats2_ok", "aggr2_ok", "var2_ok")

            def router(r):
                def wide(t):
                    return t.unsqueeze(2).to_broadcast([P, TILES, E])

                wait(dve, "logit_done", 2 * r + 1)
                dve.tensor_tensor(lg[:, 0], logit_ps.rearrange("p (s e) -> p s e", s=TILES), rb_sb.unsqueeze(1).to_broadcast([P, TILES, E]),
                                  ALU.add).then_inc(s["lg_ok"], 1)
                wait(dve, "lg_ok", r)
                dve.tensor_reduce(col[:, 0], lg[:, 0], AX_X, ALU.max).then_inc(s["lmax_ok"], 1)
                wait(dve, "lmax_ok", r)
                dve.tensor_tensor(lg[:, 1], lg[:, 0], wide(col[:, 0]), ALU.subtract).then_inc(s["shift_ok"], 1)
                wait(dve, "shift_ok", r)
                dve.scalar_tensor_tensor(lg[:, 3], lg[:, 1], 0.0, order.unsqueeze(1).to_broadcast([P, TILES, E]),
                                         ALU.is_equal, ALU.mult).then_inc(s["first_ok"], 1)
                wait(dve, "first_ok", r)
                dve.tensor_reduce(col[:, 3], lg[:, 3], AX_X, ALU.max).then_inc(s["big_ok"], 1)
                wait(dve, "big_ok", r)
                dve.wait_ge(s["tables_ok"], 1)
                wait(dve, "rank_done", r - 1)
                dve.tensor_tensor(chosen.rearrange("p (t e) -> p t e", e=E), lg[:, 3], wide(col[:, 3]), ALU.is_equal).then_inc(s["mask_ok"], 1)
                dve.wait_ge(s["zero_ok"], 2)
                for k in range(2):
                    dve.tensor_tensor(mask.rearrange("p b s e -> p (b s) e")[:, r * TILES:(r + 1) * TILES, k * E:(k + 1) * E],
                                      lg[:, 3], wide(col[:, 3]), ALU.is_equal).then_inc(s["mask_ok"], 1)

            def probabilities(r):
                wait(dve, "prob_ok", r)
                dve.tensor_reduce(col[:, 1], lg[:, 2], AX_X, ALU.add).then_inc(s["psum_ok"], 1)
                wait(dve, "psum_ok", r)
                dve.reciprocal(col[:, 2], col[:, 1]).then_inc(s["rden_ok"], 1)
                wait(dve, "rden_ok", r)
                dve.tensor_scalar(cw[:, 2 * r:2 * r + 2].rearrange("p b s -> p (b s)"), col[:, 2], tg[:, 1:2], None, ALU.mult).then_inc(s["cw_ok"], 1)

            def slots(r):
                def square(t, axis):
                    return t.unsqueeze(axis).to_broadcast([P, E, E])

                n = rank_sb[:, TILES * E:]
                cells = grid[:, 0:E * E].rearrange("p (a e) -> p a e", a=E)
                owners = grid.rearrange("p (n e) -> p n e", n=BLOCKS)
                taken = mask.rearrange("p b s e -> p (b s) e")[:, r * TILES:(r + 1) * TILES, 0:E]
                wait(dve, "mask_ok", r)
                wait(dve, "rank_done", r)
                dve.tensor_copy(rank_sb, rank_ps).then_inc(s["slot_ok"], 1)
                wait(dve, "slot_ok", r, 1)
                dve.tensor_tensor(cells, square(n, 2), square(table["step"], 1), ALU.is_gt).then_inc(s["slot_ok"], 1)
                wait(dve, "slot_ok", r, 2)
                dve.tensor_reduce(nblocks[:, 0], cells, AX_X, ALU.add).then_inc(s["slot_ok"], 1)
                wait(dve, "slot_ok", r, 3)
                dve.tensor_tensor(cells, square(nblocks[:, 0], 1), table["lower"].rearrange("p (a e) -> p a e", a=E), ALU.mult).then_inc(s["slot_ok"], 1)
                wait(dve, "slot_ok", r, 4)
                dve.tensor_reduce(nblocks[:, 1], cells, AX_X, ALU.add).then_inc(s["slot_ok"], 1)
                wait(dve, "slot_ok", r, 5)
                dve.scalar_tensor_tensor(cells, square(nblocks[:, 1], 1), float(P), rank_sb[:, 0:TILES * E].rearrange("p (t e) -> p t e", t=TILES),
                                         ALU.mult, ALU.add).then_inc(s["slot_ok"], 1)
                dve.tensor_tensor(nblocks[:, 2], nblocks[:, 1], nblocks[:, 0], ALU.add).then_inc(s["slot_ok"], 1)
                wait(dve, "slot_ok", r, 7)
                dve.tensor_tensor(cells, cells, taken, ALU.mult).then_inc(s["slot_ok"], 1)
                wait(dve, "slot_ok", r, 8)
                dve.tensor_reduce(slot[:, :], cells, AX_X, ALU.add).then_inc(s["slot_ok"], 1)
                wait(dve, "slot_ok", r, 9)
                dve.tensor_copy(index[:, r], slot[:, :]).then_inc(s["index_ok"], 1)
                dve.tensor_tensor(owners, nblocks[:, 2].unsqueeze(1).to_broadcast([P, BLOCKS, E]),
                                  table["number"].unsqueeze(2).to_broadcast([P, BLOCKS, E]), ALU.is_le).then_inc(s["slot_ok"], 1)
                wait(dve, "slot_ok", r, 10)
                dve.tensor_reduce(whose[:, :], owners, AX_X, ALU.add).then_inc(s["owner_ok"], 1)
                wait(dve, "owner_ok", r)
                dve.tensor_scalar(whose_int[:, r, 0:BLOCKS], whose[:, :], float(E - 1), None, ALU.min).then_inc(s["expert_ok"], 1)

            def biases(b):
                wait(dve, "cw_ok", b // 2)
                for t in range(S):
                    wait(dve, "ebias_done", b, t // 2 * 2 + 2)
                    dve.scalar_tensor_tensor(x_sb[:, b, t], ebias_ps[t // 2][:, t % 2 * D:t % 2 * D + D], cw[:, b, t:t + 1],
                                             x_sb[:, b, t], ALU.mult, ALU.add).then_inc(s["bias_ok"], 1)

            def blocks_low(r, k):
                wait(dve, "bhi_ok", r, k + 1)
                n = min(2, BLOCKS - 2 * k) * D
                dve.tensor_tensor(b_lo[:, k % 4, 0:n], block_ps[k % RING][:, 0:n], f32(b_hi[:, k % 4, 0:n]), ALU.subtract).then_inc(s["blo_ok"], 1)

            def add_products(r):
                for t in range(TILES):
                    b = 2 * r + t // S
                    wait(dve, "bias_ok", b, t % S + 1)
                    dve.wait_ge(gathered[r][t], 16)
                    dve.scalar_tensor_tensor(x_sb[:, b, t % S], yg[r][t], cw[:, b, t % S:t % S + 1], x_sb[:, b, t % S],
                                             ALU.mult, ALU.add).then_inc(s["sum_ok"], 1)

            x_statistics(0)
            x_roots(0)
            x_combinations(0)
            x_statistics(1)
            x_roots(1)
            x_statistics(2)
            x_combinations(1)
            x_low(0)
            x_roots(2)
            c_low(0)
            x_low(1)
            x_combinations(2)
            c_low(1)
            x_statistics(3)
            correlate(0)
            x_roots(3)
            split_experts(range(0, 2))
            x_low(2)
            x_combinations(3)
            c_low(2)
            split_experts(range(2, 4))
            correlate(1)
            split_experts(range(4, C * E // 2))
            x_low(3)
            c_low(3)
            correlation_spectra(0)
            rank(0)
            correlate(2)
            weight_combinations(0)
            split_biases()
            correlate(3)
            weights_low(0)
            convolve(0)
            correlation_spectra(1)
            convolve(1)
            rank(1)
            weight_combinations(1)
            residual(0)
            weights_low(1)
            token_variances(0)
            roots(0, "rs2_ok", "newton2_ok")
            convolve(2)
            residual(1)
            token_variances(1)
            convolve(3)
            roots(1, "rs2_ok", "newton2_ok")
            residual(2)
            token_variances(2)
            roots(2, "rs2_ok", "newton2_ok")
            router(0)
            residual(3)
            token_variances(3)
            slots(0)
            roots(3, "rs2_ok", "newton2_ok")
            probabilities(0)
            biases(0)
            router(1)
            biases(1)
            slots(1)
            probabilities(1)
            for k in range(PAIRS):
                blocks_low(0, k)
                if k == 3:
                    biases(2)
                if k == 6:
                    biases(3)
            for k in range(PAIRS):
                blocks_low(1, k)
            add_products(0)
            add_products(1)

        @block.tensor
        def _(pe):
            matmul = nc.tensor.matmul

            def keep_clock(ps, n):
                for _ in range(n):
                    matmul(ps[:, 0:P], zero[:, :], zero[:, :], start=True, stop=True)

            def transform(ps, rows, part, done):
                matmul(ps[0:rows, 2 * P:], part(2), fwd[:, 2 * P:4 * P], start=True, stop=False)
                matmul(ps[0:rows, 2 * P:], part(3), fwd[:, 4 * P:6 * P], start=False, stop=True)
                matmul(ps[0:rows, 0:P], part(0), fwd[:, 0:P], start=True, stop=True)
                matmul(ps[0:rows, P:2 * P], part(1), fwd[:, P:2 * P], start=True, stop=True).then_inc(s[done], 1)

            def project(ps, n, m, hi, lo, hi_ok, lo_ok, b, done):
                cols = slice(m * P, (m + 1) * P)
                for c in range(C):
                    wait(pe, hi_ok, b, c + 1)
                    matmul(ps[:, :], w_hi[:, n, c, cols], hi[:, c], start=(c == 0), stop=False)
                for c in range(C):
                    matmul(ps[:, :], w_lo[:, n, c, cols], hi[:, c], start=False, stop=False)
                for c in range(C):
                    wait(pe, lo_ok, b, c + 1)
                    matmul(ps[:, :], w_hi[:, n, c, cols], lo[:, c], start=False, stop=False)
                row = slice(32 * n, 32 * n + 1)
                matmul(ps[:, 0:2], bias[row, cols], crow[row, 0:2], start=False, stop=True).then_inc(s[done], 1)

            def x_spectrum(b):
                wait(pe, "xc_ok", b)
                for c in range(C):
                    wait(pe, "xlo_ok", b - 1, c + 1) if b < 3 else wait(pe, "clo_ok", b - 1, c + 1)
                    transform(x_spec_ps[c], P, lambda k: xc[:, b % 2, k, c * P:(c + 1) * P], "xspec_done")

            def c_spectrum(b):
                wait(pe, "cc_ok", b)
                for c in range(C):
                    if b >= 2:
                        wait(pe, "xlo_ok", b, c + 1)
                    transform(c_spec_ps[b][c], P, lambda k: cc[:, b % 2, k, c * P:(c + 1) * P], "cspec_done")

            def k_spectrum(b):
                for m in range(C):
                    if b >= 1:
                        wait(pe, "k_ok", b - 1, m + 1)
                    if b >= 2:
                        wait(pe, "v_ok", b - 2, m + 1)
                    project(k_ps[m], 1, m, c_hi[:, b], c_lo[:, b], "chi_ok", "clo_ok", b, "k_done")

            def q_spectrum(b):
                for m in range(C):
                    wait(pe, "clo_ok", 0, m + 1) if b == 0 else wait(pe, "m_ok", b - 1, 3 * m + 3)
                    project(q_ps[m], 0, m, x_hi[:, b % 2], x_lo[:, b % 2], "xhi_ok", "xlo_ok", b, "q_done")

            def v_spectrum(b):
                for m in range(C):
                    wait(pe, "k_ok", (1, 2, 3, 3)[b], m + 1)
                    wait(pe, "v_ok", b - 1, m + 1)
                    project(v_ps[m], 2, m, c_hi[:, b], c_lo[:, b], "chi_ok", "clo_ok", b, "v_done")

            def head_sums(b):
                wait(pe, "prod_ok", b)
                wait(pe, "clo_ok", 1)
                if b == 2:
                    wait(pe, "cspec_ok", 0)
                for c in range(C):
                    for g in range(G):
                        col = g * ROWS + b * H + c * HC
                        mm = matmul(corr_spec_ps[:, col:col + HC], prod[:, b % 2, c, g].rearrange("p r j -> p (r j)"), hones,
                                    start=True, stop=True)
                mm.then_inc(s["sum_done"], 1)

            def correlations(r):
                pe.wait_ge(s["inv_in"], 16)
                wait(pe, "cspec_ok", r)
                wait(pe, "wflo_ok", r - 1)
                for g in range(G):
                    mm = matmul(corr_ps[0:PAIR, :], corr_spec[:, g], inv[:, g], start=(g == 0), stop=(g == G - 1))
                mm.then_inc(s["corr_done"], 1)

            def turn_weights(r):
                wait(pe, "w_ok", r)
                for q in range(S):
                    mm = nc.tensor.transpose(wt_ps[:, q * PAIR:(q + 1) * PAIR], w_sb[:, q * P:(q + 1) * P], idn[0:PAIR, 0:PAIR])
                mm.then_inc(s["wt_done"], 1)

            def weight_spectrum(r):
                wait(pe, "wc_ok", r)
                transform(wf_ps, PAIR, lambda k: wc[:, k], "wf_done")

            def spread_weights(b):
                pe.wait_ge(s["pick_ok"], 1)
                wait(pe, "wflo_ok", b // 2)
                for c in range(C):
                    wait(pe, "n_ok", b - 1, 3 * c + 3)
                    matmul(wspec_ps[c][:, :], pick[:, b % 2, c], wf_hi[:, :], start=True, stop=False)
                    matmul(wspec_ps[c][:, :], pick[:, b % 2, c], wf_lo[:, :], start=False, stop=True).then_inc(s["wspec_done"], 1)

            def output_spectrum(b):
                wait(pe, "vp_ok", b)
                for h in range(2):
                    if b == 1:
                        wait(pe, "v_ok", B - 1, h + 1)
                    elif b >= 2:
                        wait(pe, ("res1_ok", "res2_ok")[h], b - 2)
                    for g in (2 * h, 2 * h + 1):
                        ps = y_ps[b][h][:, g % 2 * D:g % 2 * D + D]
                        for c in range(C):
                            mm = matmul(ps, prod[:, b % 2, c, g].rearrange("p r j -> p (r j)"), w_raw[:, 3, c],
                                        start=(c == 0), stop=(g > 0 and c == C - 1))
                        if g == 0:
                            mm = matmul(ps, crow[96:97, :], bias[96:97, :], start=False, stop=True)
                    mm.then_inc(s["y_done"], 1)

            def back_to_time(b):
                for h, (ps, done) in enumerate(((even_ps[b], "even_done"), (odd_ps[b], "odd_done"))):
                    wait(pe, "y_ok", b, h + 1)
                    for n in range(2):
                        for g in (2 * h, 2 * h + 1):
                            mm = matmul(ps[:, n * D:(n + 1) * D], inv[:, g, n * P:(n + 1) * P], y_sb[:, b % 2, g],
                                        start=(g == 2 * h), stop=(g == 2 * h + 1))
                    mm.then_inc(s[done], 1)

            def turn_tokens(b, c):
                wait(pe, "xn2_ok", b)
                wait(pe, "t_ok", b, c) if c else wait(pe, "t_ok", b - 1)
                for t in range(S):
                    mm = nc.tensor.transpose(turned_ps[:, t * P:(t + 1) * P], xn2[b][:, t, c * P:(c + 1) * P], idn)
                mm.then_inc(s["turned_done"], 1)

            def logits(b):
                wait(pe, "wflo_ok", 1)
                if b == 2:
                    wait(pe, "lg_ok", 0)
                    wait(pe, "slot_ok", 0, 1)
                wait(pe, "t_ok", b)
                for t in range(S):
                    col = (b % 2 * S + t) * E
                    for c in range(C):
                        mm = matmul(logit_ps[:, col:col + E], t_sb[b % 2][:, c, t * P:(t + 1) * P], rw_raw[:, c], start=(c == 0), stop=(c == C - 1))
                mm.then_inc(s["logit_done"], 1)

            def ranks(r):
                ps = rank_ps.rearrange("p (t e) -> p t e", e=E)
                marks = chosen.rearrange("p (t e) -> p t e", e=E)
                wait(pe, "mask_ok", r, 1)
                matmul(rank_ps, zero[:, :], tables[:, 0:(TILES + 1) * E], start=True, stop=False)
                matmul(ps[:, 0:TILES], counters[:, 0], marks, start=False, stop=False)
                for t in range(TILES):
                    mm = matmul(ps[:, t + 1:], counters[:, 1], marks[:, t].unsqueeze(1).to_broadcast([P, TILES - t, E]),
                                start=False, stop=(t == TILES - 1))
                mm.then_inc(s["rank_done"], 1)

            def turn_masks(r):
                wait(pe, "n_ok", B - 1)
                wait(pe, "bias_ok", 2 * r - 1)
                wait(pe, "mask_ok", r)
                for n in range(2):
                    mm = nc.tensor.transpose(mt_ps[:, n * P:(n + 1) * P], mask[:, 2 * r + n].rearrange("p s e -> p (s e)"), idn)
                mm.then_inc(s["mt_done"], 1)

            def expert_biases(b):
                wait(pe, "bias_ok", b - 1)
                wait(pe, "mt_ok", b // 2)
                pe.wait_ge(s["eb_ok"], 1)
                for t in range(S):
                    rows = slice(32 * t, 32 * t + 32)
                    if t % 2:
                        wait(pe, "ebias_done", b, t)
                    matmul(ebias_ps[t // 2][:, t % 2 * D:t % 2 * D + D], mt[rows, b % 2], eb_sb[rows, :], start=True, stop=True).then_inc(s["ebias_done"], 1)

            def experts_of_blocks(r):
                wait(pe, "expert_ok", r)
                _, whose = nc.values_load_multi_w_load_instructions(whose_int[0:1, r, 0:BLOCKS], engines=[pe.engine], min_val=0, max_val=E - 1,
                                                                    skip_runtime_bounds_check_because="a minimum bounds it")
                return whose

            def turn_blocks(r, k):
                if k >= RING:
                    wait(pe, "blo_ok", r, k - RING + 1)
                else:
                    wait(pe, "res2_ok", 2)
                    wait(pe, "t_ok", B - 1)
                    wait(pe, "blo_ok", r - 1)
                for n in range(2 * k, min(2 * k + 2, BLOCKS)):
                    wait(pe, f"xs_in{n // 4 % 2}", r, 16 * (n // 8 + 1))
                    for c in range(C):
                        mm = nc.tensor.transpose(block_ps[k % RING][:, (n % 2 * C + c) * P:(n % 2 * C + c + 1) * P],
                                                 xs[:, n % 8, c * P:(c + 1) * P], idn)
                mm.then_inc(s["block_turned"], 1)

            def experts(r, k, whose):
                wait(pe, "bhi_ok", r, k + 1)
                wait(pe, "blo_ok", r, k + 1)
                wait(pe, "y_out_ok", r, k - 2) if k >= RING else wait(pe, "y_out_ok", r - 1)
                if r == 0 and k < RING:
                    wait(pe, "res2_ok", 3)
                    wait(pe, "slot_ok", 1, 1)
                for n in range(2 * k, min(2 * k + 2, BLOCKS)):
                    def part(t, c):
                        return t[:, k % 4, (n % 2 * C + c) * P:(n % 2 * C + c + 1) * P]

                    def weight(w, c):
                        w = w[:, :, :].rearrange("p k (e d) -> p (k e) d", d=D)
                        return w[:, bass.ds(whose[n] + c * E, 1)].rearrange("p a d -> p (a d)")

                    terms = [(part(a, c), weight(w, c)) for c in range(C) for a, w in ((b_hi, ew_hi), (b_hi, ew_lo), (b_lo, ew_hi))]
                    for i, (a, w) in enumerate(terms):
                        mm = matmul(expert_ps[k % RING][:, n % 2 * D:n % 2 * D + D], a, w, start=(i == 0), stop=(i == len(terms) - 1))
                mm.then_inc(s["block_done"], 1)

            pe.wait_ge(s["zero_ok"], 1)
            keep_clock(bank[7], 24)
            pe.wait_ge(s["table_in"], 16)
            x_spectrum(0)
            c_spectrum(0)
            keep_clock(bank[7], 10)
            x_spectrum(1)
            pe.wait_ge(s["small_in"], 16)
            pe.wait_ge(s["wlo_ok"], 2)
            k_spectrum(0)
            c_spectrum(1)
            q_spectrum(0)
            x_spectrum(2)
            k_spectrum(1)
            c_spectrum(2)
            q_spectrum(1)
            x_spectrum(3)
            head_sums(0)
            pe.wait_ge(s["ewlo_ok"], C * E // 2)
            pe.wait_ge(s["wlo_ok"], 3)
            v_spectrum(0)
            c_spectrum(3)
            head_sums(1)
            k_spectrum(2)
            correlations(0)
            q_spectrum(2)
            v_spectrum(1)
            turn_weights(0)
            k_spectrum(3)
            q_spectrum(3)
            weight_spectrum(0)
            head_sums(2)
            spread_weights(0)
            v_spectrum(2)
            head_sums(3)
            spread_weights(1)
            correlations(1)
            v_spectrum(3)
            output_spectrum(0)
            turn_weights(1)
            back_to_time(0)
            weight_spectrum(1)
            output_spectrum(1)
            spread_weights(2)
            back_to_time(1)
            turn_tokens(0, 0)
            turn_tokens(0, 1)
            spread_weights(3)
            output_spectrum(2)
            logits(0)
            back_to_time(2)
            output_spectrum(3)
            turn_tokens(1, 0)
            back_to_time(3)
            turn_tokens(1, 1)
            logits(1)
            turn_tokens(2, 0)
            ranks(0)
            turn_tokens(2, 1)
            turn_masks(0)
            expert_biases(0)
            logits(2)
            wait(pe, "res2_ok", 2)
            keep_clock(bank[2], 5)
            turn_tokens(3, 0)
            keep_clock(bank[2], 4)
            turn_tokens(3, 1)
            keep_clock(bank[2], 4)
            logits(3)
            expert_biases(1)
            whose = [experts_of_blocks(0)]
            ranks(1)
            turn_masks(1)
            for r in range(2):
                turn_blocks(r, 0)
                turn_blocks(r, 1)
                for k in range(PAIRS):
                    if k + 2 < PAIRS:
                        turn_blocks(r, k + 2)
                    experts(r, k, whose[r])
                    if r == 0 and k == 1:
                        expert_biases(2)
                    if r == 0 and k == 4:
                        expert_biases(3)
                if r == 0:
                    whose.append(experts_of_blocks(1))


_INS = ("x", "ctx", "wqk", "wvo", "ew", "fwd_table", "inv_table", "small_in", "counts", "head_pick", "sort_tables")


def kernel(x, ctx_1024, g_xattn, g_ffn, L0_xattn_Wq, L0_xattn_bq, L0_xattn_Wk, L0_xattn_bk, L0_xattn_Wv, L0_xattn_bv,
           L0_xattn_Wo, L0_xattn_bo, L0_ffn_router_w, L0_ffn_router_b, L0_ffn_expert_w, L0_ffn_expert_b):
    import concourse.bacc as _bacc
    from concourse.bass_utils import run_bass_kernel_spmd as _run

    def turned(w):
        w = np.asarray(w)
        return w.T.reshape(C, P, w.shape[0]).transpose(1, 0, 2)

    fwd_table, inv_table = dft_tables()
    experts = np.asarray(L0_ffn_expert_w).transpose(2, 0, 1).reshape(C, P, E, D).transpose(1, 0, 2, 3).reshape(P, C * E // 2, 2 * D)
    wqk, wvo = (np.stack([turned(a), turned(b)], 1) for a, b in ((L0_xattn_Wq, L0_xattn_Wk), (L0_xattn_Wv, L0_xattn_Wo)))
    rows = np.arange(P)
    everywhere = lambda a: np.broadcast_to(np.asarray(a).reshape(1, -1), (P, np.asarray(a).size))
    attention_biases = np.repeat(np.stack([np.asarray(a) for a in (L0_xattn_bq, L0_xattn_bk, L0_xattn_bv, L0_xattn_bo)]), P // 4, 0)
    small = dict(
        hones=rows[:, None] // DK == np.arange(HC)[None],
        crow=everywhere(L * (rows == 0)),
        idn=np.eye(P),
        order=everywhere(np.arange(E, 0, -1)),
        parts=np.stack([rows % 32 // E == 0, rows % 32 // E == 1], 1),
        rb=everywhere(L0_ffn_router_b),
        gates=np.concatenate([everywhere(g_xattn), everywhere(g_ffn)], 1),
        bias=attention_biases,
        rw=turned(L0_ffn_router_w).reshape(P, C * E),
        eb=np.tile(np.asarray(L0_ffn_expert_b), (P // E, 1)))
    small = np.concatenate([small[n].astype(np.float32) for n in SMALL], 1)
    counts = np.broadcast_to(np.arange(L, dtype=np.float32), (PAIR, L))
    heads = np.arange(PAIR)[:, None, None, None] == np.arange(2)[:, None, None] * H + np.arange(C)[:, None] * HC + rows // DK
    head_pick = heads.reshape(PAIR, 2 * C * P).astype(np.float32)
    sort_tables = dict(
        before=rows[:, None] < rows,
        ones=np.ones((P, P)),
        step=everywhere(P * np.arange(E)),
        lower=everywhere(np.arange(E)[None] < np.arange(E)[:, None]),
        number=everywhere(np.arange(BLOCKS)))
    sort_tables = np.concatenate([sort_tables[n].astype(np.float32) for n in TABLES], 1)
    arrays = dict(zip(_INS, (x, ctx_1024, wqk, wvo, experts, fwd_table, inv_table, small, counts, head_pick, sort_tables)))
    arrays = {n: np.ascontiguousarray(a) for n, a in arrays.items()}
    nc = _bacc.Bacc("TRN2", target_bir_lowering=False, num_devices=1)
    aps = {n: nc.dram_tensor(n + "_dram", a.shape, mybir.dt.from_np(a.dtype), kind="ExternalInput").ap() for n, a in arrays.items()}
    out = nc.dram_tensor("out_dram", (B, L, D), F32, kind="ExternalOutput").ap()
    build(nc, **aps, out=out)
    r = _run(nc, [{n + "_dram": a for n, a in arrays.items()}], core_ids=[0])
    return r.results[0]["out_dram"]
```
